# Optimizing a Trainium2 kernel written in Bass

```python
import numpy as np
import jax
import jax.numpy as jnp

def _softmax(x, axis=-1):
    return jax.nn.softmax(x, axis=axis)

def _gelu(x):
    return jax.nn.gelu(x, approximate=True)

def _silu(x):
    return jax.nn.silu(x)

def _sigmoid(x):
    return jax.nn.sigmoid(x)

def _layernorm(x, axis=-1, eps=1e-05):
    m = jnp.mean(x, axis=axis, keepdims=True)
    v = jnp.var(x, axis=axis, keepdims=True)
    return (x - m) / jnp.sqrt(v + eps)

def _scatter_add(tgt, idx, src, axis=0):
    return tgt.at[idx].add(src)

def _segment_sum(src, seg, n):
    return jax.ops.segment_sum(src, seg, n)
kernel_name = 'mk_hybrid_d1_jaxref_r4_621779'

def setup_inputs(seed: int=0):
    np.random.seed(seed)
    _w = jnp.asarray

    def _L0_attn_a_setup():
        import jax, jax.numpy as jnp
        import numpy as np
        NUM_HEADS = 16
        HIDDEN = 256
        HEAD_DIM = HIDDEN // NUM_HEADS
        GROUP_SIZE = 64

        def _attention(q, k, v, head_dim):
            scores = jnp.einsum('bghqd,bghkd->bghqk', q, k) / head_dim ** 0.5
            w = jax.nn.softmax(scores, axis=-1)
            return jnp.einsum('bghqk,bghkd->bghqd', w, v)
        key = jax.random.key(seed)
        k1, k2, k3 = jax.random.split(key, 3)
        hidden_states = jax.random.normal(k1, (2, 2048, HIDDEN), dtype=jnp.float32)
        w_qkv = jax.random.normal(k2, (3 * HIDDEN, HIDDEN), dtype=jnp.float32) * 0.02
        b_qkv = jax.random.normal(k3, (3 * HIDDEN,), dtype=jnp.float32) * 0.02
        return {'hidden_states': hidden_states, 'w_qkv': w_qkv, 'b_qkv': b_qkv}
    _L0_attn_a_in = _L0_attn_a_setup()

    def _L0_attn_b_setup():
        import jax, jax.numpy as jnp
        import numpy as np
        HIDDEN = 256
        HEADS = 16
        BATCH = 2
        SEQ = 512
        key = jax.random.key(seed)
        k1, k2, k3 = jax.random.split(key, 3)
        x = jax.random.normal(k1, (BATCH, SEQ, HIDDEN), dtype=jnp.float32)
        w_qkv = jax.random.normal(k2, (3 * HIDDEN, HIDDEN), dtype=jnp.float32)
        w_o = jax.random.normal(k3, (HIDDEN, HIDDEN), dtype=jnp.float32)
        return {'x': x, 'w_qkv': w_qkv, 'w_o': w_o}
    _L0_attn_b_in = _L0_attn_b_setup()

    def _L0_ffn_setup():
        import jax, jax.numpy as jnp
        import numpy as np
        key = jax.random.key(seed)
        k1, k2, k3, k4 = jax.random.split(key, 4)
        B, T, M = (4, 512, 256)
        E, F = (16, 1024)
        x = jax.random.normal(k1, (B, T, M), dtype=jnp.float32) * 0.02
        Wg = jax.random.normal(k2, (M, E), dtype=jnp.float32) * 0.02
        w1 = jax.random.normal(k3, (E, M, F), dtype=jnp.float32) * 0.02
        w2 = jax.random.normal(k4, (E, F, M), dtype=jnp.float32) * 0.02
        return {'x': x, 'Wg': Wg, 'w1': w1, 'w2': w2}
    _L0_ffn_in = _L0_ffn_setup()
    _d = {'L0_attn_a_hidden_states': _L0_attn_a_in['hidden_states'], 'L0_attn_a_w_qkv': _L0_attn_a_in['w_qkv'], 'L0_attn_a_b_qkv': _L0_attn_a_in['b_qkv'], 'L0_attn_b_w_qkv': _L0_attn_b_in['w_qkv'], 'L0_attn_b_w_o': _L0_attn_b_in['w_o'], 'L0_ffn_Wg': _L0_ffn_in['Wg'], 'L0_ffn_w1': _L0_ffn_in['w1'], 'L0_ffn_w2': _L0_ffn_in['w2']}
    _x0 = _d['L0_attn_a_hidden_states']
    _d['L0_attn_a_hidden_states'] = jax.random.normal(jax.random.fold_in(jax.random.key(seed), 1), (16, 1024, 256), dtype=_x0.dtype)
    del _x0
    return _d

def reference(L0_attn_a_hidden_states, L0_attn_a_w_qkv, L0_attn_a_b_qkv, L0_attn_b_w_qkv, L0_attn_b_w_o, L0_ffn_Wg, L0_ffn_w1, L0_ffn_w2):

    def _L0_attn_a_ref(hidden_states, w_qkv, b_qkv):
        import jax, jax.numpy as jnp
        import numpy as np
        NUM_HEADS = 16
        HIDDEN = 256
        HEAD_DIM = HIDDEN // NUM_HEADS
        GROUP_SIZE = 64

        def _attention(q, k, v, head_dim):
            scores = jnp.einsum('bghqd,bghkd->bghqk', q, k) / head_dim ** 0.5
            w = jax.nn.softmax(scores, axis=-1)
            return jnp.einsum('bghqk,bghkd->bghqd', w, v)
        b, n, _ = hidden_states.shape
        h, d, G = (NUM_HEADS, HEAD_DIM, GROUP_SIZE)
        ng = n // G
        half = G // 2
        qkv = hidden_states @ w_qkv.T + b_qkv
        qkv = qkv.reshape(b, n, 3, h, d).transpose(2, 0, 3, 1, 4)
        q, k, v = (qkv[0], qkv[1], qkv[2])

        def grp(x):
            return x.reshape(b, h, ng, G, d).transpose(0, 2, 1, 3, 4)
        q, k, v = (grp(q), grp(k), grp(v))
        q1, q2 = (q[:, :, :, :half], q[:, :, :, half:])
        k1, k2 = (k[:, :, :, :half], k[:, :, :, half:])
        v1, v2 = (v[:, :, :, :half], v[:, :, :, half:])
        q2 = jnp.roll(q2, -half, axis=2)
        k2 = jnp.roll(k2, -half, axis=2)
        v2 = jnp.roll(v2, -half, axis=2)
        out1 = _attention(q1, k1, v1, d)
        out2 = _attention(q2, k2, v2, d)
        out = jnp.concatenate([out1, out2], axis=3)
        out = jnp.concatenate([out[:, :, :, :half], jnp.roll(out[:, :, :, half:], half, axis=2)], axis=3)
        out = out.transpose(0, 2, 1, 3, 4).reshape(b, n, h * d)
        return out

    def _L0_attn_b_ref(x, w_qkv, w_o):
        import jax, jax.numpy as jnp
        import numpy as np
        HIDDEN = 256
        HEADS = 16
        BATCH = 2
        SEQ = 512
        b, s, hid = x.shape
        heads = HEADS
        d = hid // heads
        qkv = x @ w_qkv.T * hid ** (-0.5)
        qkv = qkv.reshape(b, s, 3, heads, d)
        q = jnp.transpose(qkv[:, :, 0], (0, 2, 1, 3))
        k = jnp.transpose(qkv[:, :, 1], (0, 2, 1, 3))
        v = jnp.transpose(qkv[:, :, 2], (0, 2, 1, 3))
        scores = jnp.einsum('bhqd,bhkd->bhqk', q, k) * d ** (-0.5)
        attn = jax.nn.softmax(scores, axis=-1) * (s / np.sqrt(s - 1.0))
        out = jnp.einsum('bhqk,bhkd->bhqd', attn, v) * s ** (-0.5)
        out = jnp.transpose(out, (0, 2, 1, 3)).reshape(b, s, hid)
        return out @ w_o.T * hid ** (-0.5)

    def _L0_ffn_ref(x, Wg, w1, w2):
        import jax, jax.numpy as jnp
        import numpy as np
        d = x.shape[-1]
        xr = x.reshape(-1, d)
        S = xr.shape[0]
        E = Wg.shape[1]
        C = (S + E - 1) // E
        gate = jax.nn.softmax(xr @ Wg, axis=-1)
        idx = jnp.argmax(gate, axis=1)
        gates_s = jnp.take_along_axis(gate, idx[:, None], axis=1)[:, 0]
        onehot = jax.nn.one_hot(idx, E, dtype=jnp.int32)
        loc = jnp.sum((jnp.cumsum(onehot, axis=0) - 1) * onehot, axis=1)
        valid = loc < C
        loc_pad = jnp.minimum(loc, C)
        dispatched = jnp.zeros((E, C + 1, d), dtype=x.dtype).at[idx, loc_pad].set(xr)
        dispatched = dispatched[:, :C]
        h = jax.nn.relu(jnp.einsum('ecm,emf->ecf', dispatched, w1))
        expert_out = jnp.einsum('ecf,efm->ecm', h, w2)
        gathered = expert_out[idx, jnp.minimum(loc, C - 1)]
        combined = gathered * (gates_s * valid.astype(x.dtype))[:, None]
        return combined.reshape(x.shape)
    x = L0_attn_a_hidden_states
    x = x + _L0_attn_a_ref(_layernorm(x, axis=-1), L0_attn_a_w_qkv, L0_attn_a_b_qkv)
    x = x + _L0_ffn_ref(_layernorm(x, axis=-1), L0_ffn_Wg, L0_ffn_w1, L0_ffn_w2)
    x = x + _L0_attn_b_ref(_layernorm(x, axis=-1), L0_attn_b_w_qkv, L0_attn_b_w_o)
    x = x + _L0_ffn_ref(_layernorm(x, axis=-1), L0_ffn_Wg, L0_ffn_w1, L0_ffn_w2)
    return x

_drawn_inputs = setup_inputs


def setup_inputs(seed=0):
    import zlib

    import numpy as np

    out = dict(_drawn_inputs(seed))
    spreads = {}
    factors = {}
    for name, (base, spread) in spreads.items():
        noise = np.random.default_rng([zlib.crc32(name.encode()), seed]).standard_normal(out[name].shape)
        drawn = base * np.exp(spread * noise) if base else spread * noise
        out[name] = jnp.asarray(drawn.astype(out[name].dtype))
    for name, factor in factors.items():
        out[name] = (out[name] * factor).astype(out[name].dtype)
    return out
```

```python
from contextlib import ExitStack

import concourse.bass as bass
from concourse import mybir

ALU = mybir.AluOpType
ACT = mybir.ActivationFunctionType
AX_X = mybir.AxisListType.X
F32 = mybir.dt.float32
F32R = mybir.dt.float32r
BF16 = mybir.dt.bfloat16
U32 = mybir.dt.uint32
EPS = 1e-5


def tools(nc, ctx, stage):
    own = []
    def sb(name, shape, dt):
        return ctx.enter_context(nc.sbuf_tensor(f"{stage}_{name}", shape, dt))

    def ps(name, shape):
        return ctx.enter_context(nc.psum_tensor(f"{stage}_{name}", shape, F32))

    def sem(name):
        own.append(nc.alloc_semaphore(f"{stage}_{name}"))
        return own[-1]

    def give_back():
        nc.clear_and_free_semaphores(own)
        nc.all_engine_barrier()
    ctx.callback(give_back)
    return sb, ps, sem


def row(view, g):
    if isinstance(g, int):
        return view[g]
    letters = "a b c d e"[:2 * (len(view.shape) - 1) - 1]
    return view[bass.ds(g, 1)].rearrange(f"o {letters} -> (o {letters[0]}){letters[1:]}")


def after(eng, sem, value):
    if isinstance(value, int) and value <= 0:
        return
    eng.wait_ge(sem, value)


def groups(eng, n, body, apart=1):
    apart = min(apart, n // 2 - 1)
    for g in range(2 * apart):
        body(g, g % 2, g // 2)
    if n // 2 - 1 > apart:
        with eng.Fori(apart, n // 2 - 1) as i:
            body(i * 2, 0, i)
            body(i * 2 + 1, 1, i)
    body(n - 2, 0, n // 2 - 1)
    body(n - 1, 1, n // 2 - 1)


class Seq:

    def __init__(self, eng, sem, per, before=0):
        self.eng, self.sem, self.per, self.before, self.n = eng, sem, per, before, 0

    def start(self):
        self.n = 0

    def did(self, instruction):
        instruction.then_inc(self.sem, 1)
        self.n += 1

    def wait(self, g):
        self.eng.wait_ge(self.sem, self.before + self.per * g + self.n)

    def check(self):
        assert self.n == self.per, (self.n, self.per)


def three_pass(nc, out, operands, start=True, stop=True, **kw):
    last = None
    products = [p for a_hi, a_lo, b_hi, b_lo in operands for p in ((a_hi, b_hi), (a_hi, b_lo), (a_lo, b_hi))]
    for n, (a, b) in enumerate(products):
        last = nc.tensor.matmul(out, a, b, start=start and n == 0, stop=stop and n == len(products) - 1, **kw)
    return last


class Shared:

    def __init__(self, nc, ctx):
        self.ident = ctx.enter_context(nc.sbuf_tensor("ident", [128, 128], F32))
        self.eps = ctx.enter_context(nc.sbuf_tensor("eps", [128, 1], F32))
        made = ctx.enter_context(nc.semaphore("shared_made"))
        self.settled = ctx.enter_context(nc.semaphore("shared_settled"))
        with nc.Block() as block:
            @block.gpsimd
            def _(pool):
                nc.gpsimd.memset(self.eps[:], EPS)
                nc.gpsimd.memset(self.ident[:], 0.0).then_inc(made, 1)
                pool.wait_ge(made, 1)
                nc.gpsimd.affine_select(out=self.ident[:], in_=self.ident[:], compare_op=ALU.not_equal, fill=1.0,
                                        base=0, pattern=[[-1, 128]], channel_multiplier=1).then_inc(made, 1)
                pool.wait_ge(made, 2)


    def settle(self, eng):
        eng.sem_inc(self.settled, 1)


def window_attention_stage(nc, T, x, wT, bias, att):
    N, D = x.shape
    G = 512
    NG = N // G
    H, HD, W = 16, 16, 32
    NW = G // W
    xg_ = x.rearrange("(g t p) d -> g p t d", t=4, p=128)
    ag = att.rearrange("(g t p) d -> g p t d", t=4, p=128)
    with ExitStack() as ctx:
        sb, ps, sem = tools(nc, ctx, "a")
        X = [sb(f"x{s}", [128, 4, D], F32) for s in range(2)]
        AT = [sb(f"at{s}", [128, 4, D], F32) for s in range(2)]
        XN = [sb(f"xn{s}", [128, 4, D], F32) for s in range(2)]
        xhi = sb("xhi", [128, 2, G], F32R)
        xlo = sb("xlo", [128, 2, G], F32R)
        QT = [sb(f"qT{s}", [128, 2, G], F32) for s in range(2)]
        KT = sb("kT", [128, G], F32)
        KBD = [sb(f"kbd{s}", [128, 2, NW, 8, W], F32) for s in range(2)]
        VA = [sb(f"va{s}", [128, 4, H, 32], F32) for s in range(2)]
        PR = [sb(f"p{s}", [128, H, W], F32) for s in range(2)]
        PC = [sb(f"pc{s}", [128, H, W], F32) for s in range(2)]
        PT = [sb(f"pt{s}", [128, H, 128], F32) for s in range(2)]
        OT = [sb(f"oT{s}", [128, 4, 128], F32) for s in range(2)]
        O = [sb(f"o{s}", [128, H, HD], F32) for s in range(2)]
        stats = sb("stats", [128, 4, 6], F32)
        mv = sb("mv", [128, 4, 2], F32)
        std = sb("std", [128, 4], F32)
        rstd = sb("rstd", [128, 4], F32)
        mx = sb("mx", [128, H], F32)
        rden = sb("rden", [128, H], F32)
        w_raw = sb("w_raw", [128, 2, 3 * D], F32)
        w_hi = sb("w_hi", [128, 2, 3 * D], F32R)
        w_lo = sb("w_lo", [128, 2, 3 * D], F32R)
        b_col = sb("b_col", [128, 4], F32)
        b_v = sb("b_v", [128, D], F32)
        b_masked = sb("b_masked", [128, 8], F32)
        head_mask = sb("head_mask", [128, 8], F32)
        psT = ps("psT", [128, 2, G])
        psQ = [ps(f"psQ{s}", [128, G]) for s in range(2)]
        psS = [ps(f"psS{s}", [128, H, W]) for s in range(2)]
        psO = ps("psO", [128, 4, 128])
        psX = ps("psX", [128, 4, 4, 32])

        w_loaded, w_hi_ready, w_split, set_up = sem("w_loaded"), sem("w_hi_ready"), sem("w_split"), sem("set_up")
        x_loaded, att_stored = [sem("x_loaded0"), sem("x_loaded1")], [sem("att_stored0"), sem("att_stored1")]
        stats_ready, std_ready, xn_ready = sem("stats_ready"), sem("std_ready"), sem("xn_ready")
        xT_done, hi_ready, lo_ready = sem("xT_done"), sem("hi_ready"), sem("lo_ready")
        proj_done, proj_taken, keys_ready = sem("proj_done"), sem("proj_taken"), sem("keys_ready")
        s_done, s_shifted, p_ready, pc_ready = sem("s_done"), sem("s_shifted"), sem("p_ready"), sem("pc_ready")
        pt_dve_ready, pt_act_ready = sem("pt_dve_ready"), sem("pt_act_ready")
        pv_done, oT_ready, turned = sem("pv_done"), sem("oT_ready"), sem("turned")
        o_ready, o_used, dve_seq, pool_seq = sem("o_ready"), sem("o_used"), sem("dve_seq"), sem("pool_seq")
        mx_ready, rden_ready = sem("mx_ready"), sem("rden_ready")
        block = ctx.enter_context(nc.Block())

        PARTS = [(0,), (1,), (2, 3), (4, 5, 6, 7)]

        def last_ones(g, n):
            return isinstance(g, int) and g + n >= NG

        @block.sync
        def _(sp):
            sp.dma_start(w_raw[:], wT.rearrange("(k p) n -> p k n", p=128)).then_inc(w_loaded, 16)
            with nc.allow_non_contiguous_dma(reason="512 biases, once"):
                sp.dma_start(b_col[:], bias[0:2 * D].rearrange("(c p) -> p c", p=128)).then_inc(w_loaded, 16)
            sp.dma_start(b_v[:], bias[2 * D:3 * D].rearrange("(o d) -> o d", o=1).broadcast_to([128, D])).then_inc(w_loaded, 16)
            for g in range(2):
                sp.dma_start(X[g][:], xg_[g]).then_inc(x_loaded[g], 16)

            def group(g, s, i):
                if not last_ones(g, 2):
                    sp.wait_ge(xn_ready, g + 1)
                    sp.dma_start(X[s][:], row(xg_, g + 2)).then_inc(x_loaded[s], 16)
                if not (isinstance(g, int) and g == 0):
                    store(g - 1, 1 - s)

            def store(g, s):
                sp.wait_ge(o_used, 4 * g + 4)
                sp.dma_start(row(ag, g), AT[s][:]).then_inc(att_stored[s], 16)
            groups(sp, NG, group)
            store(NG - 1, 1)
            for s in range(2):
                sp.wait_ge(att_stored[s], 16 * (NG // 2))

        @block.gpsimd
        def _(pool):
            nc.gpsimd.memset(head_mask[:], 1.0).then_inc(pool_seq, 1)
            pool.wait_ge(pool_seq, 1)
            nc.gpsimd.affine_select(out=head_mask[:], in_=head_mask[:], compare_op=ALU.is_ge, fill=0.0, base=0,
                                    pattern=[[-16, 8]], channel_multiplier=1).then_inc(pool_seq, 1)
            pool.wait_ge(pool_seq, 2)
            nc.gpsimd.affine_select(out=head_mask[:], in_=head_mask[:], compare_op=ALU.is_ge, fill=0.0, base=15,
                                    pattern=[[16, 8]], channel_multiplier=-1).then_inc(pool_seq, 1)
            for s in range(2):
                nc.gpsimd.memset(PT[s][:], 0.0)
                nc.gpsimd.memset(VA[s][:], 0.0).then_inc(pool_seq, 1)
            pool.wait_ge(pool_seq, 5)
            for s in range(2):
                nc.gpsimd.memset(VA[s][:, :, :, HD:HD + 1], 1.0)
            pool.wait_ge(w_loaded, 48)
            nc.gpsimd.tensor_tensor(b_masked[:], b_col[:, 2:3].broadcast_to([128, 8]), head_mask[:], ALU.mult).then_inc(set_up, 1)

            def group(g, s, i):
                for t in range(4):
                    pool.wait_ge(o_ready, 4 * g + t + 1)
                    if t == 0:
                        after(pool, att_stored[s], 16 * i)
                    nc.gpsimd.tensor_tensor(AT[s][:, t, :].rearrange("p (a j d) -> p j a d", a=2, d=HD), O[t % 2][:].rearrange("p (j a) d -> p j a d", a=2),
                                            b_v[:].rearrange("p (j a d) -> p j a d", a=2, d=HD), ALU.add).then_inc(o_used, 1)
            groups(pool, NG, group)

        @block.scalar
        def _(act):
            act.wait_ge(set_up, 1)

            def norm_scale(g):
                act.wait_ge(stats_ready, g + 1)
                nc.scalar.activation(std[:], mv[:, :, 1], ACT.Sqrt, bias=T.eps[:]).then_inc(std_ready, 1)

            def split_hi(g):
                act.wait_ge(xT_done, g + 1)
                after(act, proj_done, 8 * g)
                nc.scalar.activation(xhi[:], psT[:], ACT.Copy).then_inc(hi_ready, 1)

            def take(g, s, part):
                act.wait_ge(proj_done, 8 * g + part + 1)
                src = psQ[part % 2]
                if part == 0:
                    after(act, s_done, 4 * (g - 1))
                    for h in range(8):
                        last = nc.scalar.activation(KBD[s][:, 0, :, h, :], src[:].rearrange("p (w k) -> p w k", w=NW),
                                                    ACT.Identity, bias=b_masked[:, h:h + 1], scale=head_mask[:, h:h + 1])
                elif part == 1:
                    after(act, keys_ready, g)
                    last = nc.scalar.activation(KT[:], src[:], ACT.Identity, bias=b_col[:, 3:4])
                elif part < 4:
                    last = nc.scalar.activation(QT[s][:, part - 2, :], src[:], ACT.Identity, bias=b_col[:, part - 2:part - 1])
                else:
                    if part == 4:
                        after(act, pv_done, 4 * (g - 1))
                    last = nc.scalar.activation(VA[s][:, part - 4, :, 0:HD], src[:, 0:D].rearrange("p (h d) -> p h d", h=H), ACT.Copy)
                last.then_inc(proj_taken, 1)

            def exps(n, b):
                act.wait_ge(s_shifted, n + 1)
                nc.scalar.activation(PR[b][:], PR[b][:], ACT.Exp, scale=HD ** -0.5).then_inc(p_ready, 1)

            def spread_weights(n, b):
                act.wait_ge(pc_ready, n + 1)
                after(act, pv_done, n - 1)
                for w in (2, 3):
                    r = slice(32 * w, 32 * w + 32)
                    last = nc.scalar.activation(PT[b][r, :, r], PC[b][r, :, :], ACT.Copy)
                last.then_inc(pt_act_ready, 1)

            def take_values(n, b):
                act.wait_ge(pv_done, n + 1)
                after(act, turned, n - 1)
                nc.scalar.activation(OT[b][:], psO[:], ACT.Copy).then_inc(oT_ready, 1)

            norm_scale(0)
            norm_scale(1)
            split_hi(0)
            for part in range(8):
                take(0, 0, part)

            def group(g, s, i):
                if not last_ones(g, 1):
                    split_hi(g + 1)
                for t in range(4):
                    n = 4 * g + t
                    if not (isinstance(g, int) and n < 1):
                        spread_weights(n - 1, (t + 1) % 2)
                    exps(n, t % 2)
                    if t > 0 and not last_ones(g, 1):
                        for part in PARTS[t]:
                            take(g + 1, 1 - s, part)
                    if not (isinstance(g, int) and n < 1):
                        take_values(n - 1, (t + 1) % 2)
                    if t == 0 and not last_ones(g, 1):
                        take(g + 1, 1 - s, 0)
                    if t == 3 and not last_ones(g, 2):
                        norm_scale(g + 2)
            groups(act, NG, group)
            spread_weights(4 * NG - 1, 1)
            take_values(4 * NG - 1, 1)

        @block.vector
        def _(dve):
            dve.wait_ge(w_loaded, 48)
            dve.wait_ge(set_up, 1)
            nc.vector.tensor_copy(w_hi[:], w_raw[:]).then_inc(w_hi_ready, 1)
            dve.wait_ge(w_hi_ready, 1)
            nc.vector.tensor_tensor(w_lo[:], w_raw[:], w_hi[:].bitcast(F32), ALU.subtract).then_inc(w_split, 1)

            def statistics(g, s, i):
                dve.wait_ge(x_loaded[s], 16 * (i + 1))
                for t in range(4):
                    last = nc.vector.bn_stats(stats[:, t, :], X[s][:, t, :])
                last.then_inc(dve_seq, 1)

            def variances(g):
                dve.wait_ge(dve_seq, 2 * g + 1)
                after(dve, std_ready, g)
                T.settle(dve)
                for t in range(4):
                    last = nc.vector.bn_aggr(mv[:, t, :], stats[:, t, :])
                last.then_inc(stats_ready, 1)

            def normal_tokens(g, s):
                dve.wait_ge(std_ready, g + 1)
                nc.vector.reciprocal(rstd[:], std[:]).then_inc(dve_seq, 1)
                dve.wait_ge(dve_seq, 2 * g + 2)
                after(dve, xT_done, g - 1)
                for t in range(4):
                    last = nc.vector.tensor_scalar(XN[s][:, t, :], X[s][:, t, :], mv[:, t, 0:1], rstd[:, t:t + 1],
                                                   ALU.subtract, ALU.mult)
                last.then_inc(xn_ready, 1)

            def split_lo(g):
                dve.wait_ge(hi_ready, g + 1)
                nc.vector.tensor_tensor(xlo[:], psT[:], xhi[:].bitcast(F32), ALU.subtract).then_inc(lo_ready, 1)

            def spread_keys(g, s):
                dve.wait_ge(proj_taken, 8 * g + 2)
                after(dve, s_done, 4 * (g - 1))
                for h in range(8):
                    last = nc.vector.tensor_scalar(KBD[s][:, 1, :, h, :], KT[:].rearrange("p (w k) -> p w k", w=NW), head_mask[:, h:h + 1], None, ALU.mult)
                last.then_inc(keys_ready, 1)

            def softmax(n, b):
                dve.wait_ge(s_done, n + 1)
                after(dve, pc_ready, n - 1)
                nc.vector.reduce_max(mx[:], psS[b][:], AX_X).then_inc(mx_ready, 1)
                dve.wait_ge(mx_ready, n + 1)
                nc.vector.tensor_tensor(PR[b][:], psS[b][:], mx[:].unsqueeze(2).broadcast_to([128, H, W]), ALU.subtract).then_inc(s_shifted, 1)

            def weights_by_key(n, b):
                dve.wait_ge(p_ready, n + 1)
                after(dve, pt_act_ready, n - 1)
                nc.vector.transpose(PC[b][:], PR[b][:]).then_inc(pc_ready, 1)
                dve.wait_ge(pc_ready, n + 1)
                after(dve, pv_done, n - 1)
                for w in (0, 1):
                    r = slice(32 * w, 32 * w + 32)
                    last = nc.vector.tensor_copy(PT[b][r, :, r], PC[b][r, :, :])
                last.then_inc(pt_dve_ready, 1)

            def divide(n, b):
                dve.wait_ge(turned, n + 1)
                nc.vector.reciprocal(rden[:].rearrange("p (c h) -> p c h", c=4), psX[:, :, :, HD]).then_inc(rden_ready, 1)
                dve.wait_ge(rden_ready, n + 1)
                after(dve, o_used, n - 1)
                nc.vector.tensor_tensor(O[b][:].rearrange("p (c h) d -> p c h d", c=4), psX[:, :, :, 0:HD],
                                        rden[:].rearrange("p (c h) -> p c h", c=4).unsqueeze(3).broadcast_to([128, 4, 4, HD]), ALU.mult).then_inc(o_ready, 1)

            for g in range(2):
                statistics(g, g, 0)
                variances(g)
                normal_tokens(g, g)
            split_lo(0)
            spread_keys(0, 0)

            def group(g, s, i):
                for t in range(4):
                    n = 4 * g + t
                    if not (isinstance(g, int) and n < 1):
                        weights_by_key(n - 1, (t + 1) % 2)
                    softmax(n, t % 2)
                    if t == 0 and not last_ones(g, 1):
                        split_lo(g + 1)
                    if t == 1 and not last_ones(g, 2):
                        statistics(g + 2, s, i + 1)
                    if t == 2:
                        if not last_ones(g, 2):
                            variances(g + 2)
                        if not last_ones(g, 1):
                            spread_keys(g + 1, 1 - s)
                    if not (isinstance(g, int) and n < 2):
                        divide(n - 2, t % 2)
                    if t == 3 and not last_ones(g, 2):
                        normal_tokens(g + 2, s)
            groups(dve, NG, group)
            weights_by_key(4 * NG - 1, 1)
            divide(4 * NG - 2, 0)
            divide(4 * NG - 1, 1)

        @block.tensor
        def _(pe):
            pe.wait_ge(w_split, 1)

            def transposes(g, s):
                pe.wait_ge(xn_ready, g + 1)
                after(pe, lo_ready, g)
                for t in range(4):
                    for k in range(2):
                        last = nc.tensor.transpose(psT[:, k, 128 * t:128 * t + 128], XN[s][:, t, 128 * k:128 * k + 128], T.ident[:])
                last.then_inc(xT_done, 1)

            def project(g, part):
                if part == 0:
                    pe.wait_ge(lo_ready, g + 1)
                after(pe, proj_taken, 8 * g + part - 1)
                if part < 4:
                    c = (2, 3, 0, 1)[part]
                    cs = slice(128 * c, 128 * c + 128)
                    three_pass(nc, psQ[part % 2][:], [(w_hi[:, k, cs], w_lo[:, k, cs], xhi[:, k, :], xlo[:, k, :]) for k in range(2)]).then_inc(proj_done, 1)
                else:
                    tok = slice(128 * (part - 4), 128 * (part - 4) + 128)
                    three_pass(nc, psQ[part % 2][:, 0:D], [(xhi[:, k, tok], xlo[:, k, tok], w_hi[:, k, 2 * D:], w_lo[:, k, 2 * D:])
                                                           for k in range(2)]).then_inc(proj_done, 1)

            def scores(g, s, t):
                if t == 0:
                    pe.wait_ge(proj_taken, 8 * g + 4)
                    pe.wait_ge(keys_ready, g + 1)
                after(pe, s_shifted, 4 * g + t - 1)
                for c in range(2):
                    for w in range(4):
                        tok = slice(128 * t + 32 * w, 128 * t + 32 * w + 32)
                        last = nc.tensor.matmul(psS[t % 2][32 * w:32 * w + 32, 8 * c:8 * c + 8, :], QT[s][:, c, tok],
                                                KBD[s][:, c, 4 * t + w, :, :], start=True, stop=True)
                last.then_inc(s_done, 1)

            def values(g, s, t):
                n = 4 * g + t
                if t == 0:
                    pe.wait_ge(proj_taken, 8 * g + 8)
                pe.wait_ge(pt_dve_ready, n + 1)
                pe.wait_ge(pt_act_ready, n + 1)
                after(pe, oT_ready, n)
                for c in range(4):
                    for h in range(4):
                        last = nc.tensor.matmul(psO[32 * h:32 * h + 32, c, :], VA[s][:, t, 4 * c + h, :], PT[t % 2][:, 4 * c + h, :],
                                                start=True, stop=True)
                last.then_inc(pv_done, 1)

            def turn(n, b):
                pe.wait_ge(oT_ready, n + 1)
                after(pe, o_ready, n)
                for c in range(4):
                    last = nc.tensor.transpose(psX[:, c, :, :], OT[b][:, c, :], T.ident[:])
                last.then_inc(turned, 1)

            transposes(0, 0)
            for part in range(8):
                project(0, part)

            def group(g, s, i):
                if not last_ones(g, 1):
                    transposes(g + 1, 1 - s)
                for t in range(4):
                    n = 4 * g + t
                    if t < 3:
                        scores(g, s, t + 1)
                    elif not last_ones(g, 1):
                        scores(g + 1, 1 - s, 0)
                    if not (isinstance(g, int) and n < 2):
                        turn(n - 2, t % 2)
                    if t > 0 and not last_ones(g, 1):
                        for part in PARTS[t]:
                            project(g + 1, part)
                    if t > 0:
                        values(g, s, t - 1)
                    elif not (isinstance(g, int) and g == 0):
                        values(g - 1, 1 - s, 3)
                    if t == 0 and not last_ones(g, 1):
                        project(g + 1, 0)
            scores(0, 0, 0)
            groups(pe, NG, group)
            turn(4 * NG - 2, 0)
            values(NG - 1, 1, 3)
            turn(4 * NG - 1, 1)


class Router:

    E = 16

    def __init__(self, nc, ctx, n_tokens):
        self.n_tiles = n_tokens // 128
        self.C = (n_tokens + self.E - 1) // self.E
        keep = lambda name, shape, dt: ctx.enter_context(nc.sbuf_tensor(f"route_{name}", shape, dt))
        self.slots = keep("slots", [128, self.n_tiles], U32)
        self.gates = keep("gates", [128, self.n_tiles], F32)
        self.tokens = keep("tokens", [128, self.n_tiles], U32)


def routing_stage(nc, T, R, stage, x, Wg, xn_out, table, att=None, x_out=None):
    N, D = x.shape
    E, C = R.E, R.C
    TI = 8 if N % 1024 == 0 else 4
    G = 128 * TI
    NG = N // G
    NONE = float(1 << 20)
    xg_ = x.rearrange("(g t p) d -> g p t d", t=TI, p=128)
    if att is not None:
        assert TI == 8
        attg = att.rearrange("(g A c) (a m) -> g a A c m", A=64, c=16, a=2)
        xog = x_out.rearrange("(g t p) d -> g p t d", t=TI, p=128)
    xng = xn_out.rearrange("(g t p) d -> g p t d", t=TI, p=128)
    with ExitStack() as ctx:
        sb, ps, sem = tools(nc, ctx, stage)
        X = [sb(f"x{s}", [128, TI, D], F32) for s in range(2)]
        XN = [sb(f"xn{s}", [128, TI, D], F32) for s in range(2)]
        xT = [sb(f"xT{s}", [128, 2, G], F32) for s in range(2)]
        if att is not None:
            A = [sb(f"att{s}", [128, 16, TI, 16], F32) for s in range(2)]
            XO = [sb(f"xo{s}", [128, TI, D], F32) for s in range(2)]
            att_loaded, xo_stored = [sem(f"att_loaded{s}") for s in range(2)], [sem(f"xo_stored{s}") for s in range(2)]
            xo_ready = sem("xo_ready")
        else:
            XO = X
        wg = sb("wg", [128, 2, E], F32)
        stats = sb("stats", [128, TI, 6], F32)
        mv = sb("mv", [128, TI, 2], F32)
        std = sb("std", [128, TI], F32)
        rstd = sb("rstd", [128, TI], F32)
        mx = sb("mx", [128, TI], F32)
        below = sb("below", [128, TI, E], F32)
        expd = sb("expd", [128, TI, E], F32)
        marks = sb("marks", [128, TI, E], F32)
        best = sb("best", [128, TI], F32)
        onehot = [sb(f"onehot{s}", [128, TI, E], BF16) for s in range(2)]
        counted = [sb(f"counted{s}", [128, E], BF16) for s in range(2)]
        count = sb("count", [128, E], F32)
        rank = sb("rank", [128, E], F32)
        first = sb("first", [128, TI], F32)
        picked = sb("picked", [128, TI, E], F32)
        place = sb("place", [128, TI], F32)
        inside = sb("inside", [128, TI], F32)
        total = sb("total", [128, TI], F32)
        gate = sb("gate", [128, TI], F32)
        spot = sb("spot", [128, TI], F32)
        target = sb("target", [128, TI], F32)
        kept = sb("kept", [128, TI], F32)
        target_row = [sb(f"target_row{s}", [128, TI], U32) for s in range(2)]
        token = [sb(f"token{s}", [128, TI], U32) for s in range(2)]
        earlier = sb("earlier", [128, 128], BF16)
        ones = sb("ones", [128, 128], BF16)
        zeros = sb("zeros", [128, E * C // 128], U32)
        psT = ps("psT", [128, 2, G])
        psL = [ps(f"psL{s}", [128, TI, E]) for s in range(2)]
        psC = [ps(f"psC{s}", [128, TI, E]) for s in range(2)]

        wg_loaded, set_up, table_clear = sem("wg_loaded"), sem("set_up"), sem("table_clear")
        x_loaded, xn_stored = [sem(f"x_loaded{s}") for s in range(2)], [sem(f"xn_stored{s}") for s in range(2)]
        scattered = [sem(f"scattered{s}") for s in range(2)]
        stats_ready, std_ready, xn_ready = sem("stats_ready"), sem("std_ready"), sem("xn_ready")
        xT_done, xT_ready, logits_done = sem("xT_done"), sem("xT_ready"), sem("logits_done")
        below_ready, exp_ready, onehot_ready, places_done = sem("below_ready"), sem("exp_ready"), sem("onehot_ready"), sem("places_done")
        targets_ready, dve_seq, pool_seq = sem("targets_ready"), sem("dve_seq"), sem("pool_seq")
        measured, rstd_ready, total_ready = sem("measured"), sem("rstd_ready"), sem("total_ready")
        block = ctx.enter_context(nc.Block())

        @block.sync
        def _(sp):
            sp.dma_start(wg[:], Wg.rearrange("(k p) e -> p k e", p=128)).then_inc(wg_loaded, 16)
            def load(g, s):
                sp.dma_start(X[s][:], row(xg_, g)).then_inc(x_loaded[s], 16)
                if att is not None:
                    for a in range(2):
                        sp.dma_start(A[s][64 * a:64 * a + 64], row(attg, g)[a].rearrange("A c (j d) -> A c j d", d=16)).then_inc(att_loaded[s], 16)
            for g in range(2):
                load(g, g)
            sp.wait_ge(set_up, 1)
            sp.dma_start(table.rearrange("(p n) o -> p (n o)", p=128), zeros[:]).then_inc(table_clear, 16)

            def group(g, s, i):
                if att is not None:
                    sp.wait_ge(xo_ready, TI * g + TI)
                    sp.dma_start(row(xog, g), XO[s][:]).then_inc(xo_stored[s], 16)
                sp.wait_ge(xn_ready, g + 1)
                sp.dma_start(row(xng, g), XN[s][:]).then_inc(xn_stored[s], 16)
                if not (isinstance(g, int) and g + 2 >= NG):
                    load(g + 2, s)
            groups(sp, NG, group)
            for s in range(2):
                sp.wait_ge(xn_stored[s], 16 * (NG // 2))
                if att is not None:
                    sp.wait_ge(xo_stored[s], 16 * (NG // 2))

        @block.gpsimd
        def _(pool):
            nc.gpsimd.memset(zeros[:], 0)
            nc.gpsimd.memset(ones[:], 1.0)
            nc.gpsimd.memset(counted[0][:], 0.0)
            nc.gpsimd.memset(earlier[:], 1.0).then_inc(pool_seq, 1)
            nc.gpsimd.iota(rank[:], pattern=[[-1, E]], base=E, channel_multiplier=0, allow_small_or_imprecise_dtypes=True)
            nc.gpsimd.iota(R.tokens[:], pattern=[[128, R.n_tiles]], base=0, channel_multiplier=1)
            pool.wait_ge(pool_seq, 1)
            nc.gpsimd.affine_select(out=earlier[:], in_=earlier[:], compare_op=ALU.is_ge, fill=0.0, base=-1,
                                    pattern=[[1, 128]], channel_multiplier=-1).then_inc(set_up, 1)
            pool.wait_ge(table_clear, 16)

            def group(g, s, i):
                pool.wait_ge(targets_ready, g + 1)
                T.settle(pool)
                for t in range(TI):
                    nc.gpsimd.indirect_dma_start(table, bass.IndirectOffsetOnAxis(ap=target_row[s][:, t:t + 1], axis=0),
                                                 token[s][:, t:t + 1], None, bounds_check=E * C - 1,
                                                 oob_is_err=False).then_inc(scattered[s], 16)
            groups(pool, NG, group)
            for s in range(2):
                pool.wait_ge(scattered[s], 16 * TI * (NG // 2))

        def next_is_there(g, n=1):
            return not (isinstance(g, int) and g + n >= NG)

        @block.scalar
        def _(act):
            def deviation(g):
                act.wait_ge(stats_ready, g + 1)
                nc.scalar.activation(std[:], mv[:, :, 1], ACT.Sqrt, bias=T.eps[:]).then_inc(std_ready, 1)

            def take_transposed(g, s):
                act.wait_ge(xT_done, g + 1)
                after(act, logits_done, g - 1)
                nc.scalar.activation(xT[s][:], psT[:], ACT.Copy).then_inc(xT_ready, 1)
            deviation(0)
            deviation(1)
            take_transposed(0, 0)

            def group(g, s, i):
                act.wait_ge(below_ready, g + 1)
                nc.scalar.activation(expd[:], below[:], ACT.Exp).then_inc(exp_ready, 1)
                if next_is_there(g):
                    take_transposed(g + 1, 1 - s)
                if next_is_there(g, 2):
                    deviation(g + 2)
            groups(act, NG, group)

        @block.vector
        def _(dve):
            dve.wait_ge(set_up, 1)
            ROUTE_OPS = 9
            seq = Seq(dve, dve_seq, ROUTE_OPS)

            def add_attention(g, s, i, t):
                if att is None or not 0 <= t < TI:
                    return
                if t == 0:
                    dve.wait_ge(x_loaded[s], 16 * (i + 1))
                    dve.wait_ge(att_loaded[s], 32 * (i + 1))
                    after(dve, xo_stored[s], 16 * i)
                nc.vector.tensor_tensor(XO[s][:, t, :].rearrange("p (c d) -> p c d", d=16), X[s][:, t, :].rearrange("p (c d) -> p c d", d=16),
                                        A[s][:, :, t, :], ALU.add).then_inc(xo_ready, 1)

            def measure(g, s, i, t):
                add_attention(g, s, i, t + 1)
                if not 0 <= t < TI:
                    return
                if att is not None:
                    dve.wait_ge(xo_ready, TI * g + t + 1)
                elif t == 0:
                    dve.wait_ge(x_loaded[s], 16 * (i + 1))
                nc.vector.bn_stats(stats[:, t, :], XO[s][:, t, :]).then_inc(measured, 1)

            def gather_statistics(g):
                dve.wait_ge(measured, TI * g + TI)
                after(dve, std_ready, g)
                T.settle(dve)
                for t in range(TI):
                    last = nc.vector.bn_aggr(mv[:, t, :], stats[:, t, :])
                last.then_inc(stats_ready, 1)

            def inverse_deviation(g):
                dve.wait_ge(std_ready, g + 1)
                nc.vector.reciprocal(rstd[:], std[:]).then_inc(rstd_ready, 1)

            def normalise(g, s, i, t):
                if t == 0:
                    dve.wait_ge(rstd_ready, g + 1)
                    after(dve, xT_done, g - 1)
                    after(dve, xn_stored[s], 16 * i)
                last = nc.vector.tensor_scalar(XN[s][:, t, :], XO[s][:, t, :], mv[:, t, 0:1], rstd[:, t:t + 1], ALU.subtract, ALU.mult)
                if t == TI - 1:
                    last.then_inc(xn_ready, 1)

            for g in range(2):
                for t in range(-1, TI):
                    measure(g, g, 0, t)
                gather_statistics(g)
                inverse_deviation(g)
                for t in range(TI):
                    normalise(g, g, 0, t)

            def group(g, s, i):
                ahead = next_is_there(g, 2)
                def tiles(step, *ts):
                    for t in ts:
                        if ahead and t < TI:
                            step(g + 2, s, i + 1, t)
                seq.start()
                bc = lambda v: v[:].unsqueeze(2).broadcast_to([128, TI, E])
                dve.wait_ge(logits_done, g + 1)
                seq.did(nc.vector.reduce_max(mx[:], psL[s][:], AX_X))
                tiles(measure, -1)
                seq.wait(g)
                after(dve, exp_ready, g)
                nc.vector.tensor_tensor(below[:], psL[s][:], bc(mx), ALU.subtract).then_inc(below_ready, 1)
                tiles(measure, 0)
                dve.wait_ge(below_ready, g + 1)
                seq.did(nc.vector.scalar_tensor_tensor(out=marks[:], in0=below[:], scalar=0.0,
                                                       in1=rank[:].unsqueeze(1).broadcast_to([128, TI, E]),
                                                       op0=ALU.is_equal, op1=ALU.mult))
                tiles(measure, 1)
                seq.wait(g)
                seq.did(nc.vector.reduce_max(best[:], marks[:], AX_X))
                tiles(measure, 2)
                seq.wait(g)
                after(dve, places_done, g - 1)
                seq.did(nc.vector.tensor_tensor(onehot[s][:], marks[:], bc(best), ALU.is_equal))
                nc.vector.tensor_scalar(first[:], best[:], -float(C), float(E * C), ALU.mult, ALU.add)
                tiles(measure, 3)
                seq.wait(g)
                seq.did(nc.vector.tensor_reduce(count[:], onehot[s][:].rearrange("p t e -> p e t"), AX_X, ALU.add))
                tiles(measure, 4)
                seq.wait(g)
                nc.vector.tensor_tensor(counted[1 - s][:], counted[s][:], count[:], ALU.add).then_inc(onehot_ready, 1)
                tiles(measure, 5, 6, 7)
                if ahead:
                    gather_statistics(g + 2)
                dve.wait_ge(exp_ready, g + 1)
                nc.vector.reduce_sum(total[:], expd[:], AX_X).then_inc(total_ready, 1)
                dve.wait_ge(places_done, g + 1)
                seq.did(nc.vector.tensor_tensor(picked[:], psC[s][:], onehot[s][:], ALU.mult))
                dve.wait_ge(total_ready, g + 1)
                nc.vector.reciprocal(gate[:], total[:])
                seq.wait(g)
                seq.did(nc.vector.reduce_sum(place[:], picked[:], AX_X))
                if ahead:
                    inverse_deviation(g + 2)
                seq.wait(g)
                nc.vector.tensor_scalar(inside[:], place[:], float(C), None, ALU.is_lt)
                nc.vector.tensor_scalar(kept[:], place[:], float(C - 1), None, ALU.min)
                seq.did(nc.vector.tensor_tensor(spot[:], first[:], place[:], ALU.add))
                tiles(normalise, 0, 1)
                seq.wait(g)
                nc.vector.tensor_scalar(target[:], inside[:], -NONE, NONE, ALU.mult, ALU.add)
                nc.vector.tensor_tensor(R.gates[:, bass.ds(g * TI, TI)], gate[:], inside[:], ALU.mult)
                after(dve, scattered[s], 16 * TI * i)
                seq.did(nc.vector.tensor_tensor(R.slots[:, bass.ds(g * TI, TI)], first[:], kept[:], ALU.add))
                nc.vector.tensor_copy(token[s][:], R.tokens[:, bass.ds(g * TI, TI)])
                tiles(normalise, 2, 3)
                seq.wait(g)
                nc.vector.tensor_tensor(target_row[s][:], target[:], spot[:], ALU.add).then_inc(targets_ready, 1)
                tiles(normalise, 4, 5, 6, 7)
                seq.check()
            groups(dve, NG, group)

        @block.tensor
        def _(pe):
            pe.wait_ge(wg_loaded, 16)
            pe.wait_ge(set_up, 1)

            def transposes(g, s):
                pe.wait_ge(xn_ready, g + 1)
                after(pe, xT_ready, g)
                for t in range(TI):
                    for k in range(2):
                        last = nc.tensor.transpose(psT[:, k, 128 * t:128 * t + 128], XN[s][:, t, 128 * k:128 * k + 128], T.ident[:])
                last.then_inc(xT_done, 1)

            def logits(g, s):
                pe.wait_ge(xT_ready, g + 1)
                after(pe, below_ready, g - 1)
                for t in range(TI):
                    for k in range(2):
                        last = nc.tensor.matmul(psL[s][:, t, :], xT[s][:, k, 128 * t:128 * t + 128], wg[:, k, :],
                                                start=k == 0, stop=k == 1)
                last.then_inc(logits_done, 1)

            def places(g, s):
                pe.wait_ge(onehot_ready, g + 1)
                after(pe, targets_ready, g - 1)
                for t in range(TI):
                    nc.tensor.matmul(psC[s][:, t, :], earlier[:], onehot[s][:, t, :], start=True, stop=False)
                    for before in range(t):
                        nc.tensor.matmul(psC[s][:, t, :], ones[:], onehot[s][:, before, :], start=False, stop=False)
                    last = nc.tensor.matmul(psC[s][:, t, :], ones[:], counted[s][:], start=False, stop=True)
                last.then_inc(places_done, 1)
            transposes(0, 0)
            logits(0, 0)

            def group(g, s, i):
                if next_is_there(g):
                    transposes(g + 1, 1 - s)
                places(g, s)
                if next_is_there(g):
                    logits(g + 1, 1 - s)
            groups(pe, NG, group)


def expert_stage(nc, T, R, stage, xn, table, w1, w2, eo):
    E, D, F = w1.shape
    C = R.C
    G = 512 if C % 1024 == 0 else C // 2
    TI = G // 128
    NG = E * C // G
    NF = F // 128
    eog = eo.rearrange("(g p t) d -> g p t d", t=TI, p=128)
    with ExitStack() as ctx:
        sb, ps, sem = tools(nc, ctx, stage)
        slot_token = sb("slot_token", [128, NG, TI], U32)
        index = [sb(f"index{s}", [128, TI], U32) for s in range(2)]
        XG = [sb(f"xg{s}", [128, TI, D], F32) for s in range(2)]
        xhi = [sb(f"xhi{s}", [128, 2, G], F32R) for s in range(2)]
        xlo = [sb(f"xlo{s}", [128, 2, G], F32R) for s in range(2)]
        w1_raw = sb("w1_raw", [128, 2, F], F32)
        w2_raw = sb("w2_raw", [128, NF, D], F32)
        w1_hi = [sb(f"w1_hi{s}", [128, 2, F], F32R) for s in range(2)]
        w1_lo = [sb(f"w1_lo{s}", [128, 2, F], F32R) for s in range(2)]
        w2_hi = [sb(f"w2_hi{s}", [128, NF, D], F32R) for s in range(2)]
        w2_lo = [sb(f"w2_lo{s}", [128, NF, D], F32R) for s in range(2)]
        h_hi = [sb(f"h_hi{s}", [128, G], F32R) for s in range(2)]
        h_lo = [sb(f"h_lo{s}", [128, G], F32R) for s in range(2)]
        EO = [sb(f"eo{s}", [128, TI, D], F32) for s in range(2)]
        psT = ps("psT", [128, 2, 512])
        psH = [ps(f"psH{s}", [128, 512]) for s in range(2)]
        psE = [ps(f"psE{s}", [128, 4, D]) for s in range(2)]

        table_loaded = sem("table_loaded")
        w_loaded, w_ready, hi_written = sem("w_loaded"), sem("w_ready"), sem("w_hi_written")
        index_ready, gathered, eo_stored = sem("index_ready"), [sem(f"gathered{s}") for s in range(2)], [sem(f"eo_stored{s}") for s in range(2)]
        xT_done, hi_ready, lo_ready = sem("xT_done"), sem("hi_ready"), sem("lo_ready")
        h_done, h_hi_ready, h_lo_ready = sem("h_done"), sem("h_hi_ready"), sem("h_lo_ready")
        h_used, eo_ready = sem("h_used"), sem("eo_ready")
        block = ctx.enter_context(nc.Block())

        def load_weights(sp, e):
            sp.dma_start(w1_raw[:], row(w1.rearrange("e (k p) f -> e p k f", p=128), e)).then_inc(w_loaded, 16)
            sp.dma_start(w2_raw[:], row(w2.rearrange("e (f p) d -> e p f d", p=128), e)).then_inc(w_loaded, 16)

        @block.sync
        def _(sp):
            sp.dma_start(slot_token[:], table.rearrange("(g p t) o -> p g (t o)", t=TI, p=128)).then_inc(table_loaded, 16)
            load_weights(sp, 0)

            def group(g, s, i):
                if s == 0 and not (isinstance(g, int) and g + 2 >= NG):
                    sp.wait_ge(w_ready, 4 * i + 4)
                    load_weights(sp, i + 1)
                sp.wait_ge(eo_ready, (TI + 1) // 2 * (g + 1))
                sp.dma_start(row(eog, g), EO[s][:]).then_inc(eo_stored[s], 16)
            groups(sp, NG, group)
            for s in range(2):
                sp.wait_ge(eo_stored[s], 16 * (NG // 2))

        @block.gpsimd
        def _(pool):
            def gather(s, i):
                for t in range(TI):
                    nc.gpsimd.indirect_dma_start(XG[s][:, t, :], None, xn,
                                                 bass.IndirectOffsetOnAxis(ap=index[s][:, t:t + 1], axis=0)).then_inc(gathered[s], 16)

            def group(g, s, i):
                pool.wait_ge(index_ready, g + 1)
                after(pool, xT_done, g - 1)
                T.settle(pool)
                gather(s, i)
            groups(pool, NG, group)

        QUARTERS = [(w1_raw, w1_hi, w1_lo, 0), (w1_raw, w1_hi, w1_lo, 1), (w2_raw, w2_hi, w2_lo, 0), (w2_raw, w2_hi, w2_lo, 1)]

        def quarter(w, part):
            return w[:, part, :] if w.shape[1] == 2 else w[:, NF // 2 * part:NF // 2 * (part + 1), :]

        def next_is_there(g, n=1):
            return not (isinstance(g, int) and g + n >= NG)

        @block.scalar
        def _(act):
            def split_x_hi(g, s):
                act.wait_ge(xT_done, g + 1)
                nc.scalar.activation(xhi[s][:], psT[:, :, 0:G], ACT.Copy).then_inc(hi_ready, 1)

            def split_w_hi(s, e, c):
                if c == 0:
                    act.wait_ge(w_loaded, 32 * e + 32)
                raw, hi, _, part = QUARTERS[c]
                nc.scalar.activation(quarter(hi[s], part), quarter(raw, part), ACT.Copy).then_inc(hi_written, 1)

            def take_outputs(g, s, i):
                act.wait_ge(h_used, NF * g + NF)
                after(act, eo_stored[s], 16 * i)
                for half in range((TI + 1) // 2):
                    rows = slice(2 * half, min(TI, 2 * half + 2))
                    nc.scalar.activation(EO[s][:, rows, :], psE[s][:, rows, :], ACT.Copy).then_inc(eo_ready, 1)

            def group(g, s, i, ws):
                for f in range(NF):
                    act.wait_ge(h_done, NF * g + f + 1)
                    after(act, h_used, NF * g + f - 1)
                    nc.scalar.activation(h_hi[f % 2][:], psH[f % 2][:, 0:G], ACT.Relu).then_inc(h_hi_ready, 1)
                    if f == 0 and not (isinstance(g, int) and g == 0):
                        take_outputs(g - 1, 1 - s, i if s == 1 else i - 1)
                    if f == 4 and next_is_there(g):
                        split_x_hi(g + 1, 1 - s)
                    if s == 1 and f in (1, 2, 3, 5) and next_is_there(g):
                        split_w_hi(1 - ws, i + 1, (1, 2, 3, 5).index(f))
            for c in range(4):
                split_w_hi(0, 0, c)
            split_x_hi(0, 0)

            def expert(e, s, i):
                group(e * 2, 0, e, s)
                group(e * 2 + 1, 1, e, s)
            groups(act, E, expert)
            take_outputs(NG - 1, 1, NG // 2 - 1)

        @block.vector
        def _(dve):
            dve.wait_ge(table_loaded, 16)
            for g in range(2):
                nc.vector.tensor_copy(index[g][:], slot_token[:, g, :]).then_inc(index_ready, 1)

            def split_x_lo(g, s):
                dve.wait_ge(hi_ready, g + 1)
                nc.vector.tensor_tensor(xlo[s][:], psT[:, :, 0:G], xhi[s][:].bitcast(F32), ALU.subtract).then_inc(lo_ready, 1)

            def split_w_lo(s, e, c):
                dve.wait_ge(hi_written, 4 * e + c + 1)
                raw, hi, lo, part = QUARTERS[c]
                nc.vector.tensor_tensor(quarter(lo[s], part), quarter(raw, part), quarter(hi[s], part).bitcast(F32),
                                        ALU.subtract).then_inc(w_ready, 1)

            def group(g, s, i, ws):
                for f in range(NF):
                    dve.wait_ge(h_hi_ready, NF * g + f + 1)
                    nc.vector.scalar_tensor_tensor(out=h_lo[f % 2][:], in0=psH[f % 2][:, 0:G], scalar=0.0,
                                                   in1=h_hi[f % 2][:].bitcast(F32), op0=ALU.max, op1=ALU.subtract).then_inc(h_lo_ready, 1)
                    if f == 0 and next_is_there(g, 2):
                        dve.wait_ge(gathered[s], 16 * TI * (i + 1))
                        nc.vector.tensor_copy(index[s][:], slot_token[:, bass.ds(g + 2, 1), :].rearrange("p o t -> p (o t)")).then_inc(index_ready, 1)
                    if s == 1 and f in (2, 3, 4, 6) and next_is_there(g):
                        split_w_lo(1 - ws, i + 1, (2, 3, 4, 6).index(f))
                    if f == 5 and next_is_there(g):
                        split_x_lo(g + 1, 1 - s)
            for c in range(4):
                split_w_lo(0, 0, c)
            split_x_lo(0, 0)

            def expert(e, s, i):
                group(e * 2, 0, e, s)
                group(e * 2 + 1, 1, e, s)
            groups(dve, E, expert)

        @block.tensor
        def _(pe):
            def transposes(g, s, i):
                pe.wait_ge(gathered[s], 16 * TI * (i + 1))
                after(pe, lo_ready, g)
                for t in range(TI):
                    for k in range(2):
                        last = nc.tensor.transpose(psT[:, k, 128 * t:128 * t + 128], XG[s][:, t, 128 * k:128 * k + 128], T.ident[:])
                last.then_inc(xT_done, 1)

            def up(g, s, i, ws, f):
                if f == 0:
                    pe.wait_ge(lo_ready, g + 1)
                    if s == 0:
                        pe.wait_ge(w_ready, 4 * i + 4)
                after(pe, h_lo_ready, NF * g + f - 1)
                fs = slice(128 * f, 128 * f + 128)
                three_pass(nc, psH[f % 2][:, 0:G], [(w1_hi[ws][:, k, fs], w1_lo[ws][:, k, fs], xhi[s][:, k, :], xlo[s][:, k, :])
                                                    for k in range(2)]).then_inc(h_done, 1)

            def down(g, s, ws, f):
                pe.wait_ge(h_lo_ready, NF * g + f + 1)
                if f == 0:
                    after(pe, eo_ready, (TI + 1) // 2 * (g - 1))
                for t in range(TI):
                    tok = slice(128 * t, 128 * t + 128)
                    last = three_pass(nc, psE[s][:, t, :], [(h_hi[f % 2][:, tok], h_lo[f % 2][:, tok], w2_hi[ws][:, f, :], w2_lo[ws][:, f, :])],
                                      start=f == 0 and t % 2 == 0, stop=f == NF - 1, skip_group_check=True)
                last.then_inc(h_used, 1)

            def group(g, s, i, ws):
                for f in range(NF):
                    if f + 1 < NF:
                        up(g, s, i, ws, f + 1)
                    elif next_is_there(g):
                        up(g + 1, 1 - s, i + s, ws if s == 0 else 1 - ws, 0)
                    if f == 2 and next_is_there(g):
                        transposes(g + 1, 1 - s, i + s)
                    down(g, s, ws, f)

            def expert(e, s, i):
                group(e * 2, 0, e, s)
                group(e * 2 + 1, 1, e, s)
            transposes(0, 0, 0)
            up(0, 0, 0, 0, 0)
            groups(pe, E, expert)


def combine_and_project_stage(nc, T, R, stage, x, eo, wT, x2, qk, v):
    N, D = x.shape
    G = 512
    NG = N // G
    H, HD = 16, 16
    xg_ = x.rearrange("(g t p) d -> g p t d", t=4, p=128)
    x2g = x2.rearrange("(g t p) d -> g p t d", t=4, p=128)
    qkb = qk.rearrange("r (b h) d n -> b r (h d) n", h=H)
    vb = v.rearrange("(b h) p k w -> b p h k w", h=H)
    with ExitStack() as ctx:
        sb, ps, sem = tools(nc, ctx, stage)
        X = [sb(f"x{s}", [128, 4, D], F32) for s in range(2)]
        EO = [sb(f"eo{s}", [128, 4, D], F32) for s in range(2)]
        X2 = [sb(f"x2{s}", [128, 4, D], F32) for s in range(2)]
        XN = [sb(f"xn{s}", [128, 4, D], F32) for s in range(2)]
        xhi = [sb(f"xhi{s}", [128, 2, G], F32R) for s in range(2)]
        xlo = [sb(f"xlo{s}", [128, 2, G], F32R) for s in range(2)]
        QKH = [sb(f"qkh{s}", [128, 4, G], F32R) for s in range(2)]
        QKL = [sb(f"qkl{s}", [128, 4, G], F32R) for s in range(2)]
        VA = [sb(f"va{s}", [128, H, 4, 32], F32) for s in range(2)]
        index = [sb(f"index{s}", [128, 4], U32) for s in range(2)]
        gate = [sb(f"gate{s}", [128, 4], F32) for s in range(2)]
        stats = sb("stats", [128, 4, 6], F32)
        mv = sb("mv", [128, 4, 2], F32)
        std = sb("std", [128, 4], F32)
        rstd = sb("rstd", [128, 4], F32)
        w_raw = sb("w_raw", [128, 2, 3 * D], F32)
        w_hi = sb("w_hi", [128, 2, 3 * D], F32R)
        w_lo = sb("w_lo", [128, 2, 3 * D], F32R)
        psT = ps("psT", [128, 2, G])
        psQ = [ps(f"psQ{s}", [128, G]) for s in range(2)]
        psV = [ps(f"psV{s}", [128, 2, D]) for s in range(2)]

        w_loaded, w_hi_ready, w_ready, set_up = sem("w_loaded"), sem("w_hi_ready"), sem("w_ready"), sem("set_up")
        x_loaded, x2_stored = [sem(f"x_loaded{s}") for s in range(2)], [sem(f"x2_stored{s}") for s in range(2)]
        gathered, qkv_stored = [sem(f"gathered{s}") for s in range(2)], [sem(f"qkv_stored{s}") for s in range(2)]
        index_ready, x2_ready = sem("index_ready"), sem("x2_ready")
        stats_ready, std_ready, xn_ready = sem("stats_ready"), sem("std_ready"), sem("xn_ready")
        xT_done, hi_ready, lo_ready = sem("xT_done"), sem("hi_ready"), sem("lo_ready")
        qk_done, qk_hi_ready, qk_lo_ready, v_done, v_ready = sem("qk_done"), sem("qk_hi_ready"), sem("qk_lo_ready"), sem("v_done"), sem("v_ready")
        gates_ready, measured, rstd_ready = sem("gates_ready"), sem("measured"), sem("rstd_ready")
        block = ctx.enter_context(nc.Block())

        def next_is_there(g, n=1):
            return not (isinstance(g, int) and g + n >= NG)

        @block.sync
        def _(sp):
            sp.dma_start(w_raw[:], wT.rearrange("(k p) n -> p k n", p=128)).then_inc(w_loaded, 16)
            for g in range(2):
                sp.dma_start(X[g][:], xg_[g]).then_inc(x_loaded[g], 16)

            def store_qkv(g, s, i):
                half = slice(G * s, G * s + G)
                sp.wait_ge(qk_lo_ready, 4 * g + 4)
                for part in range(2):
                    cs = slice(2 * part, 2 * part + 2)
                    for r, buf in ((2 * part, QKH), (2 * part + 1, QKL)):
                        sp.dma_start(row(qkb, i)[r, :, half].rearrange("(c p) n -> p c n", p=128), buf[s][:, cs, :].bitcast(F32)).then_inc(qkv_stored[s], 16)
                sp.wait_ge(v_ready, 2 * g + 2)
                sp.dma_start(row(vb, i)[:, :, 4 * s:4 * s + 4, :], VA[s][:]).then_inc(qkv_stored[s], 16)

            def group(g, s, i):
                sp.wait_ge(x2_ready, g + 1)
                sp.dma_start(row(x2g, g), X2[s][:]).then_inc(x2_stored[s], 16)
                if next_is_there(g, 2):
                    sp.dma_start(X[s][:], row(xg_, g + 2)).then_inc(x_loaded[s], 16)
                if not (isinstance(g, int) and g == 0):
                    store_qkv(g - 1, 1 - s, i if s == 1 else i - 1)
            groups(sp, NG, group)
            store_qkv(NG - 1, 1, NG // 2 - 1)
            for s in range(2):
                sp.wait_ge(x2_stored[s], 16 * (NG // 2))
                sp.wait_ge(qkv_stored[s], 80 * (NG // 2))

        @block.gpsimd
        def _(pool):
            for s in range(2):
                nc.gpsimd.memset(VA[s][:], 0.0).then_inc(set_up, 1)
            pool.wait_ge(set_up, 2)
            for s in range(2):
                nc.gpsimd.memset(VA[s][:, :, :, HD:HD + 1], 1.0).then_inc(set_up, 1)

            def group(g, s, i):
                after(pool, x2_ready, g - 1)
                after(pool, gathered[s], 64 * i)
                nc.gpsimd.tensor_copy(index[s][:], R.slots[:, bass.ds(g * 4, 4)]).then_inc(index_ready, 1)
                pool.wait_ge(index_ready, g + 1)
                T.settle(pool)
                for t in range(4):
                    nc.gpsimd.indirect_dma_start(EO[s][:, t, :], None, eo,
                                                 bass.IndirectOffsetOnAxis(ap=index[s][:, t:t + 1], axis=0)).then_inc(gathered[s], 16)
            groups(pool, NG, group)

        @block.scalar
        def _(act):
            act.wait_ge(set_up, 4)

            def deviation(g):
                act.wait_ge(stats_ready, g + 1)
                nc.scalar.activation(std[:], mv[:, :, 1], ACT.Sqrt, bias=T.eps[:]).then_inc(std_ready, 1)

            def split_hi(g, s):
                act.wait_ge(xT_done, g + 1)
                after(act, v_done, 2 * g - 2)
                nc.scalar.activation(xhi[s][:], psT[:], ACT.Copy).then_inc(hi_ready, 1)
            deviation(0)
            split_hi(0, 0)
            deviation(1)

            def group(g, s, i):
                after(act, qkv_stored[s], 80 * i)
                for c in range(4):
                    act.wait_ge(qk_done, 4 * g + c + 1)
                    nc.scalar.activation(QKH[s][:, c, :], psQ[c % 2][:], ACT.Copy, scale=D ** -0.5).then_inc(qk_hi_ready, 1)
                    if c == 2 and next_is_there(g):
                        split_hi(g + 1, 1 - s)
                for c in range(2):
                    act.wait_ge(v_done, 2 * g + c + 1)
                    nc.scalar.activation(VA[s][:, :, 2 * c:2 * c + 2, 0:HD].rearrange("p h t d -> p t h d"),
                                         psV[c][:].rearrange("p t (h d) -> p t h d", h=H), ACT.Copy, scale=D ** -0.5).then_inc(v_ready, 1)
                if next_is_there(g, 2):
                    deviation(g + 2)
            groups(act, NG, group)

        @block.vector
        def _(dve):
            dve.wait_ge(w_loaded, 16)
            nc.vector.tensor_copy(w_hi[:], w_raw[:]).then_inc(w_hi_ready, 1)
            dve.wait_ge(w_hi_ready, 1)
            nc.vector.tensor_tensor(w_lo[:], w_raw[:], w_hi[:].bitcast(F32), ALU.subtract).then_inc(w_ready, 1)

            def fetch_gates(g, s):
                after(dve, x2_ready, g - 1)
                nc.vector.tensor_copy(gate[s][:], R.gates[:, bass.ds(g * 4, 4)]).then_inc(gates_ready, 1)

            def combine(g, s, i):
                dve.wait_ge(x_loaded[s], 16 * (i + 1))
                dve.wait_ge(gathered[s], 64 * (i + 1))
                dve.wait_ge(gates_ready, g + 1)
                after(dve, x2_stored[s], 16 * i)
                for t in range(4):
                    last = nc.vector.scalar_tensor_tensor(out=X2[s][:, t, :], in0=EO[s][:, t, :], scalar=gate[s][:, t:t + 1],
                                                          in1=X[s][:, t, :], op0=ALU.mult, op1=ALU.add)
                last.then_inc(x2_ready, 1)

            def measure(g, s):
                dve.wait_ge(x2_ready, g + 1)
                for t in range(4):
                    last = nc.vector.bn_stats(stats[:, t, :], X2[s][:, t, :])
                last.then_inc(measured, 1)

            def gather_statistics(g):
                dve.wait_ge(measured, g + 1)
                after(dve, std_ready, g)
                T.settle(dve)
                for t in range(4):
                    last = nc.vector.bn_aggr(mv[:, t, :], stats[:, t, :])
                last.then_inc(stats_ready, 1)

            def normalise(g, s):
                dve.wait_ge(std_ready, g + 1)
                nc.vector.reciprocal(rstd[:], std[:]).then_inc(rstd_ready, 1)
                dve.wait_ge(rstd_ready, g + 1)
                after(dve, xT_done, g - 1)
                for t in range(4):
                    last = nc.vector.tensor_scalar(XN[s][:, t, :], X2[s][:, t, :], mv[:, t, 0:1], rstd[:, t:t + 1],
                                                   ALU.subtract, ALU.mult)
                last.then_inc(xn_ready, 1)

            def split_lo(g, s):
                dve.wait_ge(hi_ready, g + 1)
                nc.vector.tensor_tensor(xlo[s][:], psT[:], xhi[s][:].bitcast(F32), ALU.subtract).then_inc(lo_ready, 1)

            for g in range(2):
                fetch_gates(g, g)
                combine(g, g, 0)
                measure(g, g)
                if g == 1:
                    split_lo(0, 0)
                gather_statistics(g)
                if g == 0:
                    normalise(0, 0)

            def group(g, s, i):
                for c in range(4):
                    dve.wait_ge(qk_hi_ready, 4 * g + c + 1)
                    nc.vector.scalar_tensor_tensor(out=QKL[s][:, c, :], in0=psQ[c % 2][:], scalar=D ** -0.5,
                                                   in1=QKH[s][:, c, :].bitcast(F32), op0=ALU.mult, op1=ALU.subtract).then_inc(qk_lo_ready, 1)
                    if c == 0 and next_is_there(g):
                        normalise(g + 1, 1 - s)
                    if c == 1 and next_is_there(g, 2):
                        fetch_gates(g + 2, s)
                        combine(g + 2, s, i + 1)
                    if c == 2:
                        if next_is_there(g, 2):
                            measure(g + 2, s)
                        if next_is_there(g):
                            split_lo(g + 1, 1 - s)
                    if c == 3 and next_is_there(g, 2):
                        gather_statistics(g + 2)
            groups(dve, NG, group)

        @block.tensor
        def _(pe):
            pe.wait_ge(w_ready, 1)

            def transposes(g, s):
                pe.wait_ge(xn_ready, g + 1)
                after(pe, lo_ready, g)
                for t in range(4):
                    for k in range(2):
                        last = nc.tensor.transpose(psT[:, k, 128 * t:128 * t + 128], XN[s][:, t, 128 * k:128 * k + 128], T.ident[:])
                last.then_inc(xT_done, 1)
            transposes(0, 0)

            def group(g, s, i):
                pe.wait_ge(lo_ready, g + 1)
                for c in range(4):
                    after(pe, qk_lo_ready, 4 * g + c - 1)
                    three_pass(nc, psQ[c % 2][:], [(w_hi[:, k, 128 * c:128 * c + 128], w_lo[:, k, 128 * c:128 * c + 128],
                                                    xhi[s][:, k, :], xlo[s][:, k, :]) for k in range(2)]).then_inc(qk_done, 1)
                    if c == 2 and next_is_there(g):
                        transposes(g + 1, 1 - s)
                for c in range(2):
                    after(pe, v_ready, 2 * g + c - 1)
                    for t in range(2):
                        tok = slice(256 * c + 128 * t, 256 * c + 128 * t + 128)
                        last = three_pass(nc, psV[c][:, t, :], [(xhi[s][:, k, tok], xlo[s][:, k, tok], w_hi[:, k, 2 * D:], w_lo[:, k, 2 * D:])
                                                                for k in range(2)])
                    last.then_inc(v_done, 1)
            groups(pe, NG, group)


def combine_stage(nc, T, R, stage, x, eo, out):
    N, D = x.shape
    NG = N // 512
    xg_ = x.rearrange("(g t p) d -> g p t d", t=4, p=128)
    og = out.rearrange("(g t p) d -> g p t d", t=4, p=128)
    with ExitStack() as ctx:
        sb, ps, sem = tools(nc, ctx, stage)
        X = [sb(f"x{s}", [128, 4, D], F32) for s in range(2)]
        EO = [sb(f"eo{s}", [128, 4, D], F32) for s in range(2)]
        Y = [sb(f"y{s}", [128, 4, D], F32) for s in range(2)]
        index = [sb(f"index{s}", [128, 4], U32) for s in range(2)]
        gate = [sb(f"gate{s}", [128, 4], F32) for s in range(2)]
        x_loaded, stored = [sem(f"x_loaded{s}") for s in range(2)], [sem(f"stored{s}") for s in range(2)]
        gathered = [sem(f"gathered{s}") for s in range(2)]
        index_ready, y_ready = sem("index_ready"), sem("y_ready")
        block = ctx.enter_context(nc.Block())

        @block.sync
        def _(sp):
            for g in range(2):
                sp.dma_start(X[g][:], xg_[g]).then_inc(x_loaded[g], 16)

            def group(g, s, i):
                sp.wait_ge(y_ready, g + 1)
                if not (isinstance(g, int) and g + 2 >= NG):
                    sp.dma_start(X[s][:], row(xg_, g + 2)).then_inc(x_loaded[s], 16)
                sp.dma_start(row(og, g), Y[s][:]).then_inc(stored[s], 16)
            groups(sp, NG, group)
            for s in range(2):
                sp.wait_ge(stored[s], 16 * (NG // 2))

        @block.gpsimd
        def _(pool):
            def group(g, s, i):
                after(pool, y_ready, g - 1)
                pool.wait_ge(index_ready, g + 1)
                T.settle(pool)
                for t in range(4):
                    nc.gpsimd.indirect_dma_start(EO[s][:, t, :], None, eo,
                                                 bass.IndirectOffsetOnAxis(ap=index[s][:, t:t + 1], axis=0)).then_inc(gathered[s], 16)
            groups(pool, NG, group)

        @block.vector
        def _(dve):
            for g in range(2):
                nc.vector.tensor_copy(index[g][:], R.slots[:, 4 * g:4 * g + 4])
                nc.vector.tensor_copy(gate[g][:], R.gates[:, 4 * g:4 * g + 4]).then_inc(index_ready, 1)

            def group(g, s, i):
                dve.wait_ge(x_loaded[s], 16 * (i + 1))
                dve.wait_ge(gathered[s], 64 * (i + 1))
                dve.wait_ge(index_ready, g + 1)
                after(dve, stored[s], 16 * i)
                for t in range(4):
                    last = nc.vector.scalar_tensor_tensor(out=Y[s][:, t, :], in0=EO[s][:, t, :], scalar=gate[s][:, t:t + 1],
                                                          in1=X[s][:, t, :], op0=ALU.mult, op1=ALU.add)
                last.then_inc(y_ready, 1)
                if not (isinstance(g, int) and g + 2 >= NG):
                    dve.wait_ge(y_ready, g + 1)
                    nc.vector.tensor_copy(index[s][:], R.slots[:, bass.ds(g * 4 + 8, 4)])
                    nc.vector.tensor_copy(gate[s][:], R.gates[:, bass.ds(g * 4 + 8, 4)]).then_inc(index_ready, 1)
            groups(dve, NG, group)


def attention_stage(nc, T, stage, x, qk, v, woT, out):
    N, D = x.shape
    S = 1024
    B = N // S
    H, HD = 16, 16
    NH = B * H
    KC = S // 128
    MROW = 96
    OUT_SCALE = S / float(S - 1) ** 0.5 * S ** -0.5 * D ** -0.5
    xb = x.rearrange("(b t p) d -> b p t d", t=KC, p=128)
    ob = out.rearrange("(b t p) d -> b p t d", t=KC, p=128)
    qkh = qk.rearrange("r h d n -> h r d n")
    with ExitStack() as ctx:
        sb, ps, sem = tools(nc, ctx, stage)
        Q = [sb(f"q{j}", [MROW + 2, S], F32R) for j in range(4)]
        K = [sb(f"k{j}", [MROW + 2, S], F32R) for j in range(4)]
        V = [sb(f"v{j}", [128, KC, 32], F32) for j in range(4)]
        P = [sb(f"p{j}", [128, S], F32) for j in range(4)]
        best = [sb(f"best{j}", [128, KC, 2], F32) for j in range(2)]
        mx = [sb(f"mx{j}", [128, KC], F32) for j in range(2)]
        nm_hi = [sb(f"nm_hi{j}", [KC, 128], F32R) for j in range(2)]
        nm_lo = [sb(f"nm_lo{j}", [KC, 128], F32R) for j in range(2)]
        OT = sb("oT", [128, 256], F32)
        rden = sb("rden", [128, 2, 4], F32)
        O = sb("o", [128, KC, D], F32)
        oT_hi = sb("oT_hi", [128, 2, S], F32R)
        oT_lo = sb("oT_lo", [128, 2, S], F32R)
        X = sb("x", [128, KC, D], F32)
        Y = sb("y", [128, KC, D], F32)
        w_raw = sb("w_raw", [128, 2, D], F32)
        w_hi = sb("w_hi", [128, 2, D], F32R)
        w_lo = sb("w_lo", [128, 2, D], F32R)
        psM = [ps(f"psM{s}", [128, 512]) for s in range(2)]
        psE = [ps(f"psE{s}", [128, 2, 512]) for s in range(2)]
        psO = ps("psO", [128, 512])
        psX = ps("psX", [128, 512])

        w_loaded, w_hi_ready, w_ready, set_up, zeroed = sem("w_loaded"), sem("w_hi_ready"), sem("w_ready"), sem("set_up"), sem("zeroed")
        qkv_loaded = [sem(f"qkv_loaded{j}") for j in range(4)]
        max_loaded = [sem(f"max_loaded{j}") for j in range(4)]
        x_loaded, y_stored = sem("x_loaded"), sem("y_stored")
        m_done, m_taken, mx_ready = sem("m_done"), sem("m_taken"), sem("mx_ready")
        mT_done, nm_hi_ready, nm_lo_ready = sem("mT_done"), sem("nm_hi_ready"), sem("nm_lo_ready")
        e_done, p_ready, pv_done = sem("e_done"), sem("p_ready"), sem("pv_done")
        oT_ready, t_done, o_ready, rden_ready = sem("oT_ready"), sem("t_done"), sem("o_ready"), sem("rden_ready")
        xo_done, xo_hi_ready, xo_lo_ready, wo_done, y_ready = sem("xo_done"), sem("xo_hi_ready"), sem("xo_lo_ready"), sem("wo_done"), sem("y_ready")
        block = ctx.enter_context(nc.Block())

        def heads(eng, step, batch_end):
            def batch(b, last):
                first = b * 4
                step(first * 4, 0, first, 0)
                if not (isinstance(b, int) and b == 0):
                    batch_end(b - 1)
                for j in range(1, 4):
                    step(first * 4 + j, j, first, j)
                with eng.Fori(1, 3 if last else 4) as q:
                    for j in range(4):
                        step((first + q) * 4 + j, j, first + q, q * 4 + j)
                if last:
                    for j in range(4):
                        step(first * 4 + 12 + j, j, first + 3, 12 + j)
            batch(0, B == 1)
            if B > 2:
                with eng.Fori(1, B - 1) as b:
                    batch(b, False)
            if B > 1:
                batch(B - 1, True)

        @block.sync
        def _(sp):
            def load_head(hh, j):
                sp.dma_start(Q[j][0:32, :].bitcast(F32), row(qkh, hh)[0:2]).then_inc(qkv_loaded[j], 16)
                sp.dma_start(Q[j][32:48, :].bitcast(F32), row(qkh, hh)[0]).then_inc(qkv_loaded[j], 16)
                sp.dma_start(K[j][0:16, :].bitcast(F32), row(qkh, hh)[2]).then_inc(qkv_loaded[j], 16)
                sp.dma_start(K[j][16:48, :].bitcast(F32), row(qkh, hh)[2:4]).then_inc(qkv_loaded[j], 16)
                sp.dma_start(V[j][:], row(v, hh)).then_inc(qkv_loaded[j], 16)

            def load_max(hh, j):
                sp.wait_ge(nm_lo_ready, hh + 1)
                sp.dma_start(Q[j][MROW:MROW + 1, :].bitcast(F32), nm_hi[j % 2][:].bitcast(F32)).then_inc(max_loaded[j], 16)
                sp.dma_start(Q[j][MROW + 1:MROW + 2, :].bitcast(F32), nm_lo[j % 2][:].bitcast(F32)).then_inc(max_loaded[j], 16)

            sp.dma_start(w_raw[:], woT.rearrange("(k p) n -> p k n", p=128)).then_inc(w_loaded, 16)
            sp.dma_start(X[:], xb[0]).then_inc(x_loaded, 16)
            sp.wait_ge(set_up, 1)
            for h in range(3):
                load_head(h, h)
            load_max(0, 0)

            def step(hh, j, turn, h):
                if not (isinstance(hh, int) and hh + 3 >= NH):
                    after(sp, e_done, hh * KC)
                    after(sp, pv_done, hh * KC)
                    load_head(hh + 3, (j + 3) % 4)
                if not (isinstance(hh, int) and hh + 1 >= NH):
                    load_max(hh + 1, (j + 1) % 4)

            def batch_end(b):
                sp.wait_ge(y_ready, 2 * b + 2)
                sp.dma_start(row(ob, b), Y[:]).then_inc(y_stored, 16)
                if not (isinstance(b, int) and b + 1 >= B):
                    sp.dma_start(X[:], row(xb, b + 1)).then_inc(x_loaded, 16)
            heads(sp, step, batch_end)
            batch_end(B - 1)
            sp.wait_ge(y_stored, 16 * B)

        @block.gpsimd
        def _(pool):
            for j in range(4):
                nc.gpsimd.memset(Q[j][:].bitcast(F32), 0.0)
                last = nc.gpsimd.memset(K[j][:].bitcast(F32), 0.0)
            last.then_inc(zeroed, 1)
            pool.wait_ge(zeroed, 1)
            for j in range(4):
                last = nc.gpsimd.memset(K[j][MROW:MROW + 2, :].bitcast(F32), 1.0)
            last.then_inc(set_up, 1)

        @block.scalar
        def _(act):
            act.wait_ge(w_loaded, 16)
            nc.scalar.activation(w_hi[:], w_raw[:], ACT.Copy).then_inc(w_hi_ready, 1)

            def take_max(hh, j, turn):
                act.wait_ge(mT_done, hh + 1)
                after(act, max_loaded[(j + 2) % 4], (turn + 1 if j >= 2 else turn) * 32)
                nc.scalar.activation(nm_hi[j % 2][:], psX[0:KC, 256:384], ACT.Copy, scale=-1.0).then_inc(nm_hi_ready, 1)

            def exps(hh, kc):
                act.wait_ge(e_done, hh * KC + kc + 1)
                after(act, pv_done, hh * KC + kc - 3)
                nc.scalar.activation(P[kc % 4][:], psE[kc % 2][:].rearrange("p a b -> p (a b)"), ACT.Exp, scale=HD ** -0.5).then_inc(p_ready, 1)

            def take_values(hh):
                act.wait_ge(pv_done, hh * KC + KC)
                after(act, t_done, hh)
                nc.scalar.activation(OT[:], psO[:, 0:256], ACT.Copy).then_inc(oT_ready, 1)

            take_max(0, 0, 0)

            def step(hh, j, turn, h):
                for kc in range(KC):
                    exps(hh, kc)
                    if kc == 1 and not (isinstance(hh, int) and hh == 0):
                        take_values(hh - 1)
                    if kc == 0 and not (isinstance(hh, int) and hh + 1 >= NH):
                        take_max(hh + 1, (j + 1) % 4, turn if j < 3 else turn + 1)

            def batch_end(b):
                for half in range(2):
                    act.wait_ge(xo_done, 2 * b + half + 1)
                    nc.scalar.activation(oT_hi[:, :, 512 * half:512 * half + 512], psE[half][:], ACT.Copy).then_inc(xo_hi_ready, 1)
            heads(act, step, batch_end)
            take_values(NH - 1)
            batch_end(B - 1)

        @block.vector
        def _(dve):
            dve.wait_ge(w_hi_ready, 1)
            nc.vector.tensor_tensor(w_lo[:], w_raw[:], w_hi[:].bitcast(F32), ALU.subtract).then_inc(w_ready, 1)

            def maximum(hh, qt, j):
                for half in range(2):
                    dve.wait_ge(m_done, hh * (2 * KC) + 2 * qt + half + 1)
                    nc.vector.reduce_max(best[j % 2][:, qt, half:half + 1], psM[half][:], AX_X).then_inc(m_taken, 1)

            def whole_maximum(hh, j):
                dve.wait_ge(m_taken, hh * (2 * KC) + 2 * KC)
                after(dve, mT_done, hh - 1)
                nc.vector.tensor_tensor(mx[j % 2][:], best[j % 2][:, :, 0], best[j % 2][:, :, 1], ALU.max).then_inc(mx_ready, 1)

            def max_lo(hh, j):
                dve.wait_ge(nm_hi_ready, hh + 1)
                nc.vector.scalar_tensor_tensor(out=nm_lo[j % 2][:], in0=psX[0:KC, 256:384], scalar=-1.0, in1=nm_hi[j % 2][:].bitcast(F32),
                                               op0=ALU.mult, op1=ALU.subtract).then_inc(nm_lo_ready, 1)

            def normalise(hh, h):
                dve.wait_ge(t_done, hh + 1)
                tv = psX[:, 0:256].rearrange("p (c j w) -> p c j w", c=2, j=4)
                nc.vector.reciprocal(rden[:], tv[:, :, :, HD]).then_inc(rden_ready, 1)
                dve.wait_ge(rden_ready, hh + 1)
                cols = O[:, :, bass.ds(h * HD, HD)].rearrange("p (j c) d -> p c j d", c=2)
                nc.vector.tensor_tensor(cols, tv[:, :, :, 0:HD], rden[:].unsqueeze(3).broadcast_to([128, 2, 4, HD]), ALU.mult).then_inc(o_ready, 1)

            for hh in range(2):
                for qt in range(KC):
                    maximum(hh, qt, hh)
                whole_maximum(hh, hh)
                if hh == 0:
                    max_lo(0, 0)

            def step(hh, j, turn, h):
                for qt in range(KC):
                    if not (isinstance(hh, int) and hh + 2 >= NH):
                        maximum(hh + 2, qt, j)
                    if qt == 2 and not (isinstance(hh, int) and hh + 1 >= NH):
                        max_lo(hh + 1, (j + 1) % 4)
                    if qt == 4 and not (isinstance(hh, int) and hh == 0):
                        normalise(hh - 1, (h - 1) % H if isinstance(h, int) else h - 1)
                if not (isinstance(hh, int) and hh + 2 >= NH):
                    whole_maximum(hh + 2, j)

            def batch_end(b):
                for half in range(2):
                    dve.wait_ge(xo_hi_ready, 2 * b + half + 1)
                    span = slice(512 * half, 512 * half + 512)
                    nc.vector.tensor_tensor(oT_lo[:, :, span], psE[half][:], oT_hi[:, :, span].bitcast(F32), ALU.subtract).then_inc(xo_lo_ready, 1)
                dve.wait_ge(x_loaded, (b + 1) * 16)
                after(dve, y_stored, b * 16)
                for half in range(2):
                    dve.wait_ge(wo_done, 2 * b + half + 1)
                    rows = slice(4 * half, 4 * half + 4)
                    nc.vector.scalar_tensor_tensor(out=Y[:, rows, :], in0=psE[half][:].rearrange("p a (c d) -> p (a c) d", c=2), scalar=OUT_SCALE,
                                                   in1=X[:, rows, :], op0=ALU.mult, op1=ALU.add).then_inc(y_ready, 1)
            heads(dve, step, batch_end)
            normalise(NH - 1, H - 1)
            batch_end(B - 1)

        @block.tensor
        def _(pe):
            pe.wait_ge(set_up, 1)

            def scores_by_query(hh, qt, half, j, turn):
                if qt == 0 and half == 0:
                    pe.wait_ge(qkv_loaded[j], (turn + 1) * 80)
                after(pe, m_taken, hh * (2 * KC) + 2 * qt + half - 1)
                nc.tensor.matmul(psM[half][:], Q[j][0:MROW, 128 * qt:128 * qt + 128], K[j][0:MROW, 512 * half:512 * half + 512],
                                 start=True, stop=True).then_inc(m_done, 1)

            def max_rows(hh, j):
                pe.wait_ge(mx_ready, hh + 1)
                after(pe, o_ready, hh - 2)
                nc.tensor.transpose(psX[0:KC, 256:384], mx[j % 2][:], T.ident[:]).then_inc(mT_done, 1)

            def scores_by_key(hh, kc, j, turn):
                if kc == 0:
                    pe.wait_ge(max_loaded[j], (turn + 1) * 32)
                after(pe, p_ready, hh * KC + kc - 1)
                for half in range(2):
                    last = nc.tensor.matmul(psE[kc % 2][:, half, :], K[j][:, 128 * kc:128 * kc + 128], Q[j][:, 512 * half:512 * half + 512],
                                            start=True, stop=True)
                last.then_inc(e_done, 1)

            def values(hh, kc, j):
                pe.wait_ge(p_ready, hh * KC + kc + 1)
                if kc == 0:
                    after(pe, oT_ready, hh)
                for quarter in range(4):
                    last = nc.tensor.matmul(psO[32 * quarter:32 * quarter + 32, 0:256], V[j][:, kc, :], P[kc % 4][:, 256 * quarter:256 * quarter + 256],
                                            start=kc == 0, stop=kc == KC - 1)
                last.then_inc(pv_done, 1)

            def turn_values(hh):
                pe.wait_ge(oT_ready, hh + 1)
                if not (isinstance(hh, int) and hh + 2 >= NH):
                    pe.wait_ge(nm_lo_ready, hh + 3)
                after(pe, o_ready, hh)
                for c in range(2):
                    last = nc.tensor.transpose(psX[:, 128 * c:128 * c + 128], OT[:, 128 * c:128 * c + 128], T.ident[:])
                last.then_inc(t_done, 1)

            for hh in range(2):
                for qt in range(KC):
                    for half in range(2):
                        scores_by_query(hh, qt, half, hh, 0)
                if hh == 0:
                    max_rows(0, 0)

            def step(hh, j, turn, h):
                for kc in range(KC):
                    ahead = not (isinstance(hh, int) and hh + 2 >= NH)
                    if ahead:
                        scores_by_query(hh + 2, kc, 0, (j + 2) % 4, turn if j < 2 else turn + 1)
                    scores_by_key(hh, kc, j, turn)
                    if ahead:
                        scores_by_query(hh + 2, kc, 1, (j + 2) % 4, turn if j < 2 else turn + 1)
                    if kc >= 2:
                        values(hh, kc - 2, j)
                    elif not (isinstance(hh, int) and hh == 0):
                        values(hh - 1, KC - 2 + kc, (j + 3) % 4)
                    if kc == 0 and not (isinstance(hh, int) and hh + 1 >= NH):
                        max_rows(hh + 1, (j + 1) % 4)
                    if kc == 3 and not (isinstance(hh, int) and hh == 0):
                        turn_values(hh - 1)

            def batch_end(b):
                pe.wait_ge(o_ready, (b + 1) * H)
                pe.wait_ge(p_ready, (b + 1) * (H * KC) + (KC if not (isinstance(b, int) and b == B - 1) else 0))
                for half in range(2):
                    for t in range(4):
                        for k in range(2):
                            last = nc.tensor.transpose(psE[half][:, k, 128 * t:128 * t + 128], O[:, 4 * half + t, 128 * k:128 * k + 128], T.ident[:])
                    last.then_inc(xo_done, 1)
                for half in range(2):
                    pe.wait_ge(xo_lo_ready, 2 * b + half + 1)
                    if half == 0:
                        pe.wait_ge(w_ready, 1)
                    for t in range(4):
                        tok = slice(512 * half + 128 * t, 512 * half + 128 * t + 128)
                        last = three_pass(nc, psE[half][:, t // 2, 256 * (t % 2):256 * (t % 2) + 256],
                                          [(oT_hi[:, k, tok], oT_lo[:, k, tok], w_hi[:, k, :], w_lo[:, k, :]) for k in range(2)])
                    last.then_inc(wo_done, 1)
                pe.wait_ge(y_ready, 2 * b + 2)
            heads(pe, step, batch_end)
            values(NH - 1, KC - 2, 3)
            values(NH - 1, KC - 1, 3)
            turn_values(NH - 1)
            batch_end(B - 1)


def hybrid_kernel(nc, x, wqkv_aT, bqkv_a, wqkv_bT, woT, wg, w1, w2, out):
    N, D = x.shape
    H, S = 16, 1024
    NH = N // S * H
    EC = w1.shape[0] * ((N + w1.shape[0] - 1) // w1.shape[0])

    def scratch(name, shape, dt=F32):
        return nc.dram_tensor(f"scratch_{name}", shape, dt, kind="Internal").ap()
    att, x1, x2, x3, xn = (scratch(n, [N, D]) for n in ("att", "x1", "x2", "x3", "xn"))
    table, eo = scratch("table", [EC, 1], U32), scratch("eo", [EC, D])
    qk, v = scratch("qk", [4, NH, 16, S]), scratch("v", [NH, 128, S // 128, 32])
    with ExitStack() as ctx:
        T = Shared(nc, ctx)
        R = Router(nc, ctx, N)
        window_attention_stage(nc, T, x, wqkv_aT, bqkv_a, att)
        routing_stage(nc, T, R, "r1", x, wg, xn, table, att, x1)
        expert_stage(nc, T, R, "e1", xn, table, w1, w2, eo)
        combine_and_project_stage(nc, T, R, "cp", x1, eo, wqkv_bT, x2, qk, v)
        attention_stage(nc, T, "at", x2, qk, v, woT, x3)
        routing_stage(nc, T, R, "r2", x3, wg, xn, table)
        expert_stage(nc, T, R, "e2", xn, table, w1, w2, eo)
        combine_stage(nc, T, R, "co", x3, eo, out)


def kernel(L0_attn_a_hidden_states, L0_attn_a_w_qkv, L0_attn_a_b_qkv, L0_attn_b_w_qkv, L0_attn_b_w_o, L0_ffn_Wg,
           L0_ffn_w1, L0_ffn_w2):
    import numpy as np
    import concourse.bacc as bacc
    from concourse.bass_utils import run_bass_kernel_spmd

    shape = L0_attn_a_hidden_states.shape
    arrays = {
        "x": np.ascontiguousarray(L0_attn_a_hidden_states).reshape(-1, shape[-1]),
        "wqkv_aT": np.ascontiguousarray(np.asarray(L0_attn_a_w_qkv).T),
        "bqkv_a": np.ascontiguousarray(L0_attn_a_b_qkv),
        "wqkv_bT": np.ascontiguousarray(np.asarray(L0_attn_b_w_qkv).T),
        "woT": np.ascontiguousarray(np.asarray(L0_attn_b_w_o).T),
        "wg": np.ascontiguousarray(L0_ffn_Wg),
        "w1": np.ascontiguousarray(L0_ffn_w1),
        "w2": np.ascontiguousarray(L0_ffn_w2),
    }
    nc = bacc.Bacc("TRN2", target_bir_lowering=False, num_devices=1)
    args = [nc.dram_tensor(f"in_{n}", a.shape, mybir.dt.from_np(a.dtype), kind="ExternalInput").ap() for n, a in arrays.items()]
    out = nc.dram_tensor("out_x", arrays["x"].shape, F32, kind="ExternalOutput").ap()
    hybrid_kernel(nc, *args, out)
    result = run_bass_kernel_spmd(nc, [{f"in_{n}": a for n, a in arrays.items()}], core_ids=[0])
    return result.results[0]["out_x"].reshape(shape)
```

```python
from contextlib import ExitStack

import concourse.bass as bass
from concourse import mybir

ALU = mybir.AluOpType
ACT = mybir.ActivationFunctionType
AX_X = mybir.AxisListType.X
F32 = mybir.dt.float32
F32R = mybir.dt.float32r
BF16 = mybir.dt.bfloat16
U32 = mybir.dt.uint32
EPS = 1e-5


def tools(nc, ctx, stage):
    own = []
    def sb(name, shape, dt):
        return ctx.enter_context(nc.sbuf_tensor(f"{stage}_{name}", shape, dt))

    def ps(name, shape):
        return ctx.enter_context(nc.psum_tensor(f"{stage}_{name}", shape, F32))

    def sem(name):
        own.append(nc.alloc_semaphore(f"{stage}_{name}"))
        return own[-1]

    def give_back():
        nc.clear_and_free_semaphores(own)
        nc.all_engine_barrier()
    ctx.callback(give_back)
    return sb, ps, sem


def row(view, g):
    if isinstance(g, int):
        return view[g]
    letters = "a b c d e"[:2 * (len(view.shape) - 1) - 1]
    return view[bass.ds(g, 1)].rearrange(f"o {letters} -> (o {letters[0]}){letters[1:]}")


def after(eng, sem, value):
    if isinstance(value, int) and value <= 0:
        return
    eng.wait_ge(sem, value)


def groups(eng, n, body, apart=1):
    apart = min(apart, n // 2 - 1)
    for g in range(2 * apart):
        body(g, g % 2, g // 2)
    if n // 2 - 1 > apart:
        with eng.Fori(apart, n // 2 - 1) as i:
            body(i * 2, 0, i)
            body(i * 2 + 1, 1, i)
    body(n - 2, 0, n // 2 - 1)
    body(n - 1, 1, n // 2 - 1)


class Seq:

    def __init__(self, eng, sem, per, before=0):
        self.eng, self.sem, self.per, self.before, self.n = eng, sem, per, before, 0

    def start(self):
        self.n = 0

    def did(self, instruction):
        instruction.then_inc(self.sem, 1)
        self.n += 1

    def wait(self, g):
        self.eng.wait_ge(self.sem, self.before + self.per * g + self.n)

    def check(self):
        assert self.n == self.per, (self.n, self.per)


def three_pass(nc, out, operands, start=True, stop=True, **kw):
    last = None
    products = [p for a_hi, a_lo, b_hi, b_lo in operands for p in ((a_hi, b_hi), (a_hi, b_lo), (a_lo, b_hi))]
    for n, (a, b) in enumerate(products):
        last = nc.tensor.matmul(out, a, b, start=start and n == 0, stop=stop and n == len(products) - 1, **kw)
    return last


class Shared:

    def __init__(self, nc, ctx):
        self.ident = ctx.enter_context(nc.sbuf_tensor("ident", [128, 128], F32))
        self.eps = ctx.enter_context(nc.sbuf_tensor("eps", [128, 1], F32))
        made = ctx.enter_context(nc.semaphore("shared_made"))
        self.settled = ctx.enter_context(nc.semaphore("shared_settled"))
        with nc.Block() as block:
            @block.gpsimd
            def _(pool):
                nc.gpsimd.memset(self.eps[:], EPS)
                nc.gpsimd.memset(self.ident[:], 0.0).then_inc(made, 1)
                pool.wait_ge(made, 1)
                nc.gpsimd.affine_select(out=self.ident[:], in_=self.ident[:], compare_op=ALU.not_equal, fill=1.0,
                                        base=0, pattern=[[-1, 128]], channel_multiplier=1).then_inc(made, 1)
                pool.wait_ge(made, 2)


    def settle(self, eng):
        eng.sem_inc(self.settled, 1)


def window_attention_stage(nc, T, x, wT, bias, att):
    N, D = x.shape
    G = 512
    NG = N // G
    H, HD, W = 16, 16, 32
    NW = G // W
    xg_ = x.rearrange("(g t p) d -> g p t d", t=4, p=128)
    ag = att.rearrange("(g t p) d -> g p t d", t=4, p=128)
    with ExitStack() as ctx:
        sb, ps, sem = tools(nc, ctx, "a")
        X = [sb(f"x{s}", [128, 4, D], F32) for s in range(2)]
        AT = [sb(f"at{s}", [128, 4, D], F32) for s in range(2)]
        XN = [sb(f"xn{s}", [128, 4, D], F32) for s in range(2)]
        xhi = sb("xhi", [128, 2, G], F32R)
        xlo = sb("xlo", [128, 2, G], F32R)
        QT = [sb(f"qT{s}", [128, 2, G], F32) for s in range(2)]
        KT = sb("kT", [128, 2, G], F32)
        KBD = [sb(f"kbd{s}", [128, 2, NW, 8, W], F32) for s in range(2)]
        VA = [sb(f"va{s}", [128, 4, H, 32], F32) for s in range(2)]
        PR = [sb(f"p{s}", [128, H, W], F32) for s in range(2)]
        PC = [sb(f"pc{s}", [128, H, W], F32) for s in range(2)]
        PT = [sb(f"pt{s}", [128, H, 128], F32) for s in range(2)]
        OT = [sb(f"oT{s}", [128, 4, 128], F32) for s in range(2)]
        O = [sb(f"o{s}", [128, H, HD], F32) for s in range(2)]
        stats = sb("stats", [128, 4, 6], F32)
        mv = sb("mv", [128, 4, 2], F32)
        std = sb("std", [128, 4], F32)
        rstd = sb("rstd", [128, 4], F32)
        mx = sb("mx", [128, H], F32)
        rden = sb("rden", [128, H], F32)
        w_raw = sb("w_raw", [128, 2, 3 * D], F32)
        w_hi = sb("w_hi", [128, 2, 3 * D], F32R)
        w_lo = sb("w_lo", [128, 2, 3 * D], F32R)
        b_col = sb("b_col", [128, 4], F32)
        b_v = sb("b_v", [128, D], F32)
        head_mask = sb("head_mask", [128, 8], F32)
        psT = ps("psT", [128, 2, G])
        psQ = [ps(f"psQ{s}", [128, G]) for s in range(2)]
        psS = [ps(f"psS{s}", [128, H, W]) for s in range(2)]
        psO = ps("psO", [128, 4, 128])
        psX = ps("psX", [128, 4, 4, 32])

        w_loaded, w_hi_ready, w_split, set_up = sem("w_loaded"), sem("w_hi_ready"), sem("w_split"), sem("set_up")
        x_loaded, att_stored = [sem("x_loaded0"), sem("x_loaded1")], [sem("att_stored0"), sem("att_stored1")]
        stats_ready, std_ready, xn_ready = sem("stats_ready"), sem("std_ready"), sem("xn_ready")
        xT_done, hi_ready, lo_ready = sem("xT_done"), sem("hi_ready"), sem("lo_ready")
        proj_done, proj_taken, keys_ready = sem("proj_done"), sem("proj_taken"), sem("keys_ready")
        s_done, s_shifted, p_ready, pc_ready = sem("s_done"), sem("s_shifted"), sem("p_ready"), sem("pc_ready")
        pt_dve_ready, pt_act_ready = sem("pt_dve_ready"), sem("pt_act_ready")
        pv_done, oT_ready, turned = sem("pv_done"), sem("oT_ready"), sem("turned")
        o_ready, o_used, dve_seq, pool_seq = sem("o_ready"), sem("o_used"), sem("dve_seq"), sem("pool_seq")
        first_keys_ready = sem("first_keys_ready")
        mx_ready, rden_ready = sem("mx_ready"), sem("rden_ready")
        block = ctx.enter_context(nc.Block())

        PARTS = [(0,), (1, 2), (3, 4), (5, 6, 7)]
        KEYS = [(), (), (0, 5), (5, 8)]

        def last_ones(g, n):
            return isinstance(g, int) and g + n >= NG

        @block.sync
        def _(sp):
            sp.dma_start(w_raw[:], wT.rearrange("(k p) n -> p k n", p=128)).then_inc(w_loaded, 16)
            with nc.allow_non_contiguous_dma(reason="512 biases, once"):
                sp.dma_start(b_col[:], bias[0:2 * D].rearrange("(c p) -> p c", p=128)).then_inc(w_loaded, 16)
            sp.dma_start(b_v[:], bias[2 * D:3 * D].rearrange("(o d) -> o d", o=1).broadcast_to([128, D])).then_inc(w_loaded, 16)
            for g in range(2):
                sp.dma_start(X[g][:], xg_[g]).then_inc(x_loaded[g], 16)

            def group(g, s, i):
                if not last_ones(g, 2):
                    sp.wait_ge(xn_ready, g + 1)
                    sp.dma_start(X[s][:], row(xg_, g + 2)).then_inc(x_loaded[s], 16)
                if not (isinstance(g, int) and g == 0):
                    store(g - 1, 1 - s)

            def store(g, s):
                sp.wait_ge(o_used, 4 * g + 4)
                sp.dma_start(row(ag, g), AT[s][:]).then_inc(att_stored[s], 16)
            groups(sp, NG, group)
            store(NG - 1, 1)
            for s in range(2):
                sp.wait_ge(att_stored[s], 16 * (NG // 2))

        @block.gpsimd
        def _(pool):
            nc.gpsimd.memset(head_mask[:], 1.0).then_inc(pool_seq, 1)
            pool.wait_ge(pool_seq, 1)
            nc.gpsimd.affine_select(out=head_mask[:], in_=head_mask[:], compare_op=ALU.is_ge, fill=0.0, base=0,
                                    pattern=[[-16, 8]], channel_multiplier=1).then_inc(pool_seq, 1)
            pool.wait_ge(pool_seq, 2)
            nc.gpsimd.affine_select(out=head_mask[:], in_=head_mask[:], compare_op=ALU.is_ge, fill=0.0, base=15,
                                    pattern=[[16, 8]], channel_multiplier=-1).then_inc(pool_seq, 1)
            for s in range(2):
                nc.gpsimd.memset(PT[s][:], 0.0)
                nc.gpsimd.memset(VA[s][:], 0.0).then_inc(pool_seq, 1)
            pool.wait_ge(pool_seq, 5)
            for s in range(2):
                nc.gpsimd.memset(VA[s][:, :, :, HD:HD + 1], 1.0).then_inc(set_up, 1)
            pool.wait_ge(w_loaded, 48)
            def group(g, s, i):
                for t in range(4):
                    pool.wait_ge(o_ready, 4 * g + t + 1)
                    if t == 0:
                        after(pool, att_stored[s], 16 * i)
                    nc.gpsimd.tensor_tensor(AT[s][:, t, :].rearrange("p (a j d) -> p j a d", a=2, d=HD), O[t % 2][:].rearrange("p (j a) d -> p j a d", a=2),
                                            b_v[:].rearrange("p (j a d) -> p j a d", a=2, d=HD), ALU.add).then_inc(o_used, 1)
            groups(pool, NG, group)

        @block.scalar
        def _(act):
            act.wait_ge(set_up, 2)

            def norm_scale(g):
                act.wait_ge(stats_ready, g + 1)
                nc.scalar.activation(std[:], mv[:, :, 1], ACT.Sqrt, bias=T.eps[:]).then_inc(std_ready, 1)

            def split_hi(g):
                act.wait_ge(xT_done, g + 1)
                after(act, proj_done, 8 * g)
                nc.scalar.activation(xhi[:], psT[:], ACT.Copy).then_inc(hi_ready, 1)

            def take(g, s, part):
                act.wait_ge(proj_done, 8 * g + part + 1)
                src = psQ[part % 2]
                if part < 2:
                    if part == 1:
                        after(act, keys_ready, g)
                    last = nc.scalar.activation(KT[:, part, :], src[:], ACT.Identity, bias=b_col[:, 2 + part:3 + part])
                elif part < 4:
                    last = nc.scalar.activation(QT[s][:, part - 2, :], src[:], ACT.Identity, bias=b_col[:, part - 2:part - 1])
                else:
                    if part == 4:
                        after(act, pv_done, 4 * (g - 1))
                    last = nc.scalar.activation(VA[s][:, part - 4, :, 0:HD], src[:, 0:D].rearrange("p (h d) -> p h d", h=H), ACT.Copy)
                last.then_inc(proj_taken, 1)

            def spread_keys(g, s, heads):
                if heads[0] == 0:
                    act.wait_ge(proj_taken, 8 * g + 1)
                    after(act, s_done, 4 * (g - 1))
                for h in range(*heads):
                    last = nc.scalar.activation(KBD[s][:, 0, :, h, :], KT[:, 0, :].rearrange("p (w k) -> p w k", w=NW), ACT.Copy,
                                                scale=head_mask[:, h:h + 1])
                if heads[1] == 8:
                    last.then_inc(first_keys_ready, 1)

            def exps(n, b):
                act.wait_ge(s_shifted, n + 1)
                nc.scalar.activation(PR[b][:], PR[b][:], ACT.Exp, scale=HD ** -0.5).then_inc(p_ready, 1)

            def spread_weights(n, b):
                act.wait_ge(pc_ready, n + 1)
                after(act, pv_done, n - 1)
                for w in (2, 3):
                    r = slice(32 * w, 32 * w + 32)
                    last = nc.scalar.activation(PT[b][r, :, r], PC[b][r, :, :], ACT.Copy)
                last.then_inc(pt_act_ready, 1)

            def take_values(n, b):
                act.wait_ge(pv_done, n + 1)
                after(act, turned, n - 1)
                nc.scalar.activation(OT[b][:], psO[:], ACT.Copy).then_inc(oT_ready, 1)

            norm_scale(0)
            norm_scale(1)
            split_hi(0)
            for part in range(8):
                take(0, 0, part)
            spread_keys(0, 0, (0, 8))

            def group(g, s, i):
                for t in range(4):
                    n = 4 * g + t
                    ahead = not last_ones(g, 1)
                    def takes(*parts):
                        for part in parts:
                            if ahead:
                                take(g + 1, 1 - s, part)

                    def keys(*heads):
                        if ahead:
                            spread_keys(g + 1, 1 - s, heads)
                    if not (isinstance(g, int) and n < 1):
                        spread_weights(n - 1, (t + 1) % 2)
                    if t == 0 and ahead:
                        split_hi(g + 1)
                    if t == 3:
                        takes(5, 6)
                    if t == 3 and not last_ones(g, 2):
                        norm_scale(g + 2)
                    exps(n, t % 2)
                    if t == 1:
                        takes(1)
                        keys(0, 2)
                        takes(2)
                    if t == 2:
                        takes(3)
                        keys(4, 6)
                        takes(4)
                    if t == 3:
                        takes(7)
                    if not (isinstance(g, int) and n < 1):
                        take_values(n - 1, (t + 1) % 2)
                    if t == 0:
                        takes(0)
                    if t == 1:
                        keys(2, 4)
                    if t == 2:
                        keys(6, 8)
            groups(act, NG, group)
            spread_weights(4 * NG - 1, 1)
            take_values(4 * NG - 1, 1)

        @block.vector
        def _(dve):
            dve.wait_ge(w_loaded, 48)
            dve.wait_ge(set_up, 2)
            nc.vector.tensor_copy(w_hi[:], w_raw[:]).then_inc(w_hi_ready, 1)
            dve.wait_ge(w_hi_ready, 1)
            nc.vector.tensor_tensor(w_lo[:], w_raw[:], w_hi[:].bitcast(F32), ALU.subtract).then_inc(w_split, 1)

            def statistics(g, s, i):
                dve.wait_ge(x_loaded[s], 16 * (i + 1))
                for t in range(4):
                    last = nc.vector.bn_stats(stats[:, t, :], X[s][:, t, :])
                last.then_inc(dve_seq, 1)

            def variances(g):
                dve.wait_ge(dve_seq, 2 * g + 1)
                after(dve, std_ready, g)
                T.settle(dve)
                for t in range(4):
                    last = nc.vector.bn_aggr(mv[:, t, :], stats[:, t, :])
                last.then_inc(stats_ready, 1)

            def normal_tokens(g, s):
                dve.wait_ge(std_ready, g + 1)
                nc.vector.reciprocal(rstd[:], std[:]).then_inc(dve_seq, 1)
                dve.wait_ge(dve_seq, 2 * g + 2)
                after(dve, xT_done, g - 1)
                for t in range(4):
                    last = nc.vector.tensor_scalar(XN[s][:, t, :], X[s][:, t, :], mv[:, t, 0:1], rstd[:, t:t + 1],
                                                   ALU.subtract, ALU.mult)
                last.then_inc(xn_ready, 1)

            def split_lo(g):
                dve.wait_ge(hi_ready, g + 1)
                nc.vector.tensor_tensor(xlo[:], psT[:], xhi[:].bitcast(F32), ALU.subtract).then_inc(lo_ready, 1)

            def spread_keys(g, s, heads):
                if heads[0] == 0:
                    dve.wait_ge(proj_taken, 8 * g + 2)
                    after(dve, s_done, 4 * (g - 1))
                for h in range(*heads):
                    last = nc.vector.tensor_scalar(KBD[s][:, 1, :, h, :], KT[:, 1, :].rearrange("p (w k) -> p w k", w=NW), head_mask[:, h:h + 1], None, ALU.mult)
                if heads[1] == 8:
                    last.then_inc(keys_ready, 1)

            def softmax(n, b):
                dve.wait_ge(s_done, n + 1)
                after(dve, pc_ready, n - 1)
                nc.vector.reduce_max(mx[:], psS[b][:], AX_X).then_inc(mx_ready, 1)
                dve.wait_ge(mx_ready, n + 1)
                nc.vector.tensor_tensor(PR[b][:], psS[b][:], mx[:].unsqueeze(2).broadcast_to([128, H, W]), ALU.subtract).then_inc(s_shifted, 1)

            def weights_by_key(n, b):
                dve.wait_ge(p_ready, n + 1)
                after(dve, pt_act_ready, n - 1)
                nc.vector.transpose(PC[b][:], PR[b][:]).then_inc(pc_ready, 1)
                dve.wait_ge(pc_ready, n + 1)
                after(dve, pv_done, n - 1)
                for w in (0, 1):
                    r = slice(32 * w, 32 * w + 32)
                    last = nc.vector.tensor_copy(PT[b][r, :, r], PC[b][r, :, :])
                last.then_inc(pt_dve_ready, 1)

            def divide(n, b):
                dve.wait_ge(turned, n + 1)
                nc.vector.reciprocal(rden[:].rearrange("p (c h) -> p c h", c=4), psX[:, :, :, HD]).then_inc(rden_ready, 1)
                dve.wait_ge(rden_ready, n + 1)
                after(dve, o_used, n - 1)
                nc.vector.tensor_tensor(O[b][:].rearrange("p (c h) d -> p c h d", c=4), psX[:, :, :, 0:HD],
                                        rden[:].rearrange("p (c h) -> p c h", c=4).unsqueeze(3).broadcast_to([128, 4, 4, HD]), ALU.mult).then_inc(o_ready, 1)

            for g in range(2):
                statistics(g, g, 0)
                variances(g)
                normal_tokens(g, g)
            split_lo(0)
            spread_keys(0, 0, (0, 8))

            def group(g, s, i):
                for t in range(4):
                    n = 4 * g + t
                    if not (isinstance(g, int) and n < 1):
                        weights_by_key(n - 1, (t + 1) % 2)
                    softmax(n, t % 2)
                    if t == 0 and not last_ones(g, 1):
                        split_lo(g + 1)
                    if t == 1 and not last_ones(g, 2):
                        statistics(g + 2, s, i + 1)
                    if t == 2:
                        if not last_ones(g, 2):
                            variances(g + 2)
                    if KEYS[t] and not last_ones(g, 1):
                        spread_keys(g + 1, 1 - s, KEYS[t])
                    if not (isinstance(g, int) and n < 2):
                        divide(n - 2, t % 2)
                    if t == 3 and not last_ones(g, 2):
                        normal_tokens(g + 2, s)
            groups(dve, NG, group)
            weights_by_key(4 * NG - 1, 1)
            divide(4 * NG - 2, 0)
            divide(4 * NG - 1, 1)

        @block.tensor
        def _(pe):
            pe.wait_ge(w_split, 1)

            def transposes(g, s):
                pe.wait_ge(xn_ready, g + 1)
                after(pe, lo_ready, g)
                for t in range(4):
                    for k in range(2):
                        last = nc.tensor.transpose(psT[:, k, 128 * t:128 * t + 128], XN[s][:, t, 128 * k:128 * k + 128], T.ident[:])
                last.then_inc(xT_done, 1)

            def project(g, part):
                if part == 0:
                    pe.wait_ge(lo_ready, g + 1)
                after(pe, proj_taken, 8 * g + part - 1)
                if part < 4:
                    c = (2, 3, 0, 1)[part]
                    cs = slice(128 * c, 128 * c + 128)
                    three_pass(nc, psQ[part % 2][:], [(w_hi[:, k, cs], w_lo[:, k, cs], xhi[:, k, :], xlo[:, k, :]) for k in range(2)]).then_inc(proj_done, 1)
                else:
                    tok = slice(128 * (part - 4), 128 * (part - 4) + 128)
                    three_pass(nc, psQ[part % 2][:, 0:D], [(xhi[:, k, tok], xlo[:, k, tok], w_hi[:, k, 2 * D:], w_lo[:, k, 2 * D:])
                                                           for k in range(2)]).then_inc(proj_done, 1)

            def scores(g, s, t):
                if t == 0:
                    pe.wait_ge(proj_taken, 8 * g + 4)
                    pe.wait_ge(first_keys_ready, g + 1)
                    pe.wait_ge(keys_ready, g + 1)
                after(pe, s_shifted, 4 * g + t - 1)
                for c in range(2):
                    for w in range(4):
                        tok = slice(128 * t + 32 * w, 128 * t + 32 * w + 32)
                        last = nc.tensor.matmul(psS[t % 2][32 * w:32 * w + 32, 8 * c:8 * c + 8, :], QT[s][:, c, tok],
                                                KBD[s][:, c, 4 * t + w, :, :], start=True, stop=True)
                last.then_inc(s_done, 1)

            def values(g, s, t):
                n = 4 * g + t
                if t == 0:
                    pe.wait_ge(proj_taken, 8 * g + 8)
                pe.wait_ge(pt_dve_ready, n + 1)
                pe.wait_ge(pt_act_ready, n + 1)
                after(pe, oT_ready, n)
                for c in range(4):
                    for h in range(4):
                        last = nc.tensor.matmul(psO[32 * h:32 * h + 32, c, :], VA[s][:, t, 4 * c + h, :], PT[t % 2][:, 4 * c + h, :],
                                                start=True, stop=True)
                last.then_inc(pv_done, 1)

            def turn(n, b):
                pe.wait_ge(oT_ready, n + 1)
                after(pe, o_ready, n)
                for c in range(4):
                    last = nc.tensor.transpose(psX[:, c, :, :], OT[b][:, c, :], T.ident[:])
                last.then_inc(turned, 1)

            transposes(0, 0)
            for part in range(8):
                project(0, part)

            def group(g, s, i):
                for t in range(4):
                    n = 4 * g + t
                    if t < 3:
                        scores(g, s, t + 1)
                    if t == 0 and not last_ones(g, 1):
                        transposes(g + 1, 1 - s)
                    if not (isinstance(g, int) and n < 2):
                        turn(n - 2, t % 2)
                    if t > 0 and not last_ones(g, 1):
                        for part in PARTS[t]:
                            project(g + 1, part)
                    if t == 3 and not last_ones(g, 1):
                        scores(g + 1, 1 - s, 0)
                    if t > 0:
                        values(g, s, t - 1)
                    elif not (isinstance(g, int) and g == 0):
                        values(g - 1, 1 - s, 3)
                    if t == 0 and not last_ones(g, 1):
                        project(g + 1, 0)
            scores(0, 0, 0)
            groups(pe, NG, group)
            turn(4 * NG - 2, 0)
            values(NG - 1, 1, 3)
            turn(4 * NG - 1, 1)


class Router:

    E = 16

    def __init__(self, nc, ctx, n_tokens):
        self.n_tiles = n_tokens // 128
        self.C = (n_tokens + self.E - 1) // self.E
        self.tokens = ctx.enter_context(nc.sbuf_tensor("route_tokens", [128, self.n_tiles], U32))


def routing_stage(nc, T, R, stage, x, Wg, table, att=None, x_out=None):
    N, D = x.shape
    E, C = R.E, R.C
    TI = 8 if N % 1024 == 0 else 4
    G = 128 * TI
    NG = N // G
    NONE = float(1 << 20)
    xg_ = x.rearrange("(g t p) d -> g p t d", t=TI, p=128)
    if att is not None:
        assert TI == 8
        attg = att.rearrange("(g A c) (a m) -> g a A c m", A=64, c=16, a=2)
        xog = x_out.rearrange("(g t p) d -> g p t d", t=TI, p=128)
    with ExitStack() as ctx:
        sb, ps, sem = tools(nc, ctx, stage)
        X = [sb(f"x{s}", [128, TI, D], F32) for s in range(2)]
        XN = [sb(f"xn{s}", [128, TI, D], F32) for s in range(2)]
        xT = [sb(f"xT{s}", [128, 2, G], F32) for s in range(2)]
        if att is not None:
            A = [sb(f"att{s}", [128, 16, TI, 16], F32) for s in range(2)]
            XO = [sb(f"xo{s}", [128, TI, D], F32) for s in range(2)]
            att_loaded, xo_stored = [sem(f"att_loaded{s}") for s in range(2)], [sem(f"xo_stored{s}") for s in range(2)]
            xo_ready = sem("xo_ready")
        else:
            XO = X
        wg = sb("wg", [128, 2, E], F32)
        stats = sb("stats", [128, TI, 6], F32)
        mv = sb("mv", [128, TI, 2], F32)
        std = sb("std", [128, TI], F32)
        rstd = sb("rstd", [128, TI], F32)
        mx = sb("mx", [128, TI], F32)
        below = sb("below", [128, TI, E], F32)
        expd = sb("expd", [128, TI, E], F32)
        marks = sb("marks", [128, TI, E], F32)
        best = sb("best", [128, TI], F32)
        onehot = [sb(f"onehot{s}", [128, TI, E], BF16) for s in range(2)]
        counted = [sb(f"counted{s}", [128, E], BF16) for s in range(2)]
        count = sb("count", [128, E], F32)
        rank = sb("rank", [128, E], F32)
        first = sb("first", [128, TI], F32)
        picked = sb("picked", [128, TI, E], F32)
        place = sb("place", [128, TI], F32)
        inside = sb("inside", [128, TI], F32)
        total = sb("total", [128, TI], F32)
        spot = sb("spot", [128, TI], F32)
        target = sb("target", [128, TI], F32)
        target_row = [sb(f"target_row{s}", [128, TI], U32) for s in range(2)]
        entry = [sb(f"entry{s}", [128, TI, 2], U32) for s in range(2)]
        earlier = sb("earlier", [128, 128], BF16)
        ones = sb("ones", [128, 128], BF16)
        blank = sb("blank", [128, E * C // 128, 2], U32)
        psT = ps("psT", [128, 2, G])
        psL = [ps(f"psL{s}", [128, TI, E]) for s in range(2)]
        psC = [ps(f"psC{s}", [128, TI, E]) for s in range(2)]

        wg_loaded, set_up, table_clear = sem("wg_loaded"), sem("set_up"), sem("table_clear")
        x_loaded = [sem(f"x_loaded{s}") for s in range(2)]
        scattered = [sem(f"scattered{s}") for s in range(2)]
        stats_ready, std_ready, xn_ready = sem("stats_ready"), sem("std_ready"), sem("xn_ready")
        xT_done, xT_ready, logits_done = sem("xT_done"), sem("xT_ready"), sem("logits_done")
        below_ready, exp_ready, onehot_ready, places_done = sem("below_ready"), sem("exp_ready"), sem("onehot_ready"), sem("places_done")
        targets_ready, dve_seq, pool_seq = sem("targets_ready"), sem("dve_seq"), sem("pool_seq")
        measured, rstd_ready, total_ready = sem("measured"), sem("rstd_ready"), sem("total_ready")
        block = ctx.enter_context(nc.Block())

        @block.sync
        def _(sp):
            sp.dma_start(wg[:], Wg.rearrange("(k p) e -> p k e", p=128)).then_inc(wg_loaded, 16)
            def load(g, s):
                sp.dma_start(X[s][:], row(xg_, g)).then_inc(x_loaded[s], 16)
                if att is not None:
                    for a in range(2):
                        sp.dma_start(A[s][64 * a:64 * a + 64], row(attg, g)[a].rearrange("A c (j d) -> A c j d", d=16)).then_inc(att_loaded[s], 16)
            for g in range(2):
                load(g, g)
            sp.wait_ge(set_up, 1)
            sp.dma_start(table.rearrange("(p n) o -> p n o", p=128), blank[:]).then_inc(table_clear, 16)

            def group(g, s, i):
                if att is not None:
                    sp.wait_ge(xo_ready, TI * g + TI)
                    sp.dma_start(row(xog, g), XO[s][:]).then_inc(xo_stored[s], 16)
                if not (isinstance(g, int) and g + 2 >= NG):
                    sp.wait_ge(xn_ready, g + 1)
                    load(g + 2, s)
            groups(sp, NG, group)
            for s in range(2):
                if att is not None:
                    sp.wait_ge(xo_stored[s], 16 * (NG // 2))

        @block.gpsimd
        def _(pool):
            nc.gpsimd.memset(blank[:, :, 0:1], N)
            nc.gpsimd.memset(blank[:, :, 1:2], 0)
            nc.gpsimd.memset(ones[:], 1.0)
            nc.gpsimd.memset(counted[0][:], 0.0)
            nc.gpsimd.memset(earlier[:], 1.0).then_inc(pool_seq, 1)
            nc.gpsimd.iota(rank[:], pattern=[[-1, E]], base=E, channel_multiplier=0, allow_small_or_imprecise_dtypes=True)
            nc.gpsimd.iota(R.tokens[:], pattern=[[128, R.n_tiles]], base=0, channel_multiplier=1)
            pool.wait_ge(pool_seq, 1)
            nc.gpsimd.affine_select(out=earlier[:], in_=earlier[:], compare_op=ALU.is_ge, fill=0.0, base=-1,
                                    pattern=[[1, 128]], channel_multiplier=-1).then_inc(set_up, 1)
            pool.wait_ge(table_clear, 16)

            def group(g, s, i):
                pool.wait_ge(targets_ready, g + 1)
                T.settle(pool)
                for t in range(TI):
                    nc.gpsimd.indirect_dma_start(table, bass.IndirectOffsetOnAxis(ap=target_row[s][:, t:t + 1], axis=0),
                                                 entry[s][:, t, :], None, bounds_check=E * C - 1,
                                                 oob_is_err=False).then_inc(scattered[s], 16)
            groups(pool, NG, group)
            for s in range(2):
                pool.wait_ge(scattered[s], 16 * TI * (NG // 2))

        def next_is_there(g, n=1):
            return not (isinstance(g, int) and g + n >= NG)

        @block.scalar
        def _(act):
            def deviation(g):
                act.wait_ge(stats_ready, g + 1)
                nc.scalar.activation(std[:], mv[:, :, 1], ACT.Sqrt, bias=T.eps[:]).then_inc(std_ready, 1)

            def take_transposed(g, s):
                act.wait_ge(xT_done, g + 1)
                after(act, logits_done, g - 1)
                nc.scalar.activation(xT[s][:], psT[:], ACT.Copy).then_inc(xT_ready, 1)
            deviation(0)
            deviation(1)
            take_transposed(0, 0)

            def group(g, s, i):
                act.wait_ge(below_ready, g + 1)
                nc.scalar.activation(expd[:], below[:], ACT.Exp).then_inc(exp_ready, 1)
                if next_is_there(g):
                    take_transposed(g + 1, 1 - s)
                if next_is_there(g, 2):
                    deviation(g + 2)
            groups(act, NG, group)

        @block.vector
        def _(dve):
            dve.wait_ge(set_up, 1)
            ROUTE_OPS = 9
            seq = Seq(dve, dve_seq, ROUTE_OPS)

            def add_attention(g, s, i, t):
                if att is None or not 0 <= t < TI:
                    return
                if t == 0:
                    dve.wait_ge(x_loaded[s], 16 * (i + 1))
                    dve.wait_ge(att_loaded[s], 32 * (i + 1))
                    after(dve, xo_stored[s], 16 * i)
                nc.vector.tensor_tensor(XO[s][:, t, :].rearrange("p (c d) -> p c d", d=16), X[s][:, t, :].rearrange("p (c d) -> p c d", d=16),
                                        A[s][:, :, t, :], ALU.add).then_inc(xo_ready, 1)

            def measure(g, s, i, t):
                add_attention(g, s, i, t + 1)
                if not 0 <= t < TI:
                    return
                if att is not None:
                    dve.wait_ge(xo_ready, TI * g + t + 1)
                elif t == 0:
                    dve.wait_ge(x_loaded[s], 16 * (i + 1))
                nc.vector.bn_stats(stats[:, t, :], XO[s][:, t, :]).then_inc(measured, 1)

            def gather_statistics(g):
                dve.wait_ge(measured, TI * g + TI)
                after(dve, std_ready, g)
                T.settle(dve)
                for t in range(TI):
                    last = nc.vector.bn_aggr(mv[:, t, :], stats[:, t, :])
                last.then_inc(stats_ready, 1)

            def inverse_deviation(g):
                dve.wait_ge(std_ready, g + 1)
                nc.vector.reciprocal(rstd[:], std[:]).then_inc(rstd_ready, 1)

            def normalise(g, s, i, t):
                if t == 0:
                    dve.wait_ge(rstd_ready, g + 1)
                    after(dve, xT_done, g - 1)
                last = nc.vector.tensor_scalar(XN[s][:, t, :], XO[s][:, t, :], mv[:, t, 0:1], rstd[:, t:t + 1], ALU.subtract, ALU.mult)
                if t == TI - 1:
                    last.then_inc(xn_ready, 1)

            for g in range(2):
                for t in range(-1, TI):
                    measure(g, g, 0, t)
                gather_statistics(g)
                inverse_deviation(g)
                for t in range(TI):
                    normalise(g, g, 0, t)

            def group(g, s, i):
                ahead = next_is_there(g, 2)
                def tiles(step, *ts):
                    for t in ts:
                        if ahead and t < TI:
                            step(g + 2, s, i + 1, t)
                seq.start()
                bc = lambda v: v[:].unsqueeze(2).broadcast_to([128, TI, E])
                dve.wait_ge(logits_done, g + 1)
                seq.did(nc.vector.reduce_max(mx[:], psL[s][:], AX_X))
                tiles(measure, -1)
                seq.wait(g)
                after(dve, exp_ready, g)
                nc.vector.tensor_tensor(below[:], psL[s][:], bc(mx), ALU.subtract).then_inc(below_ready, 1)
                tiles(measure, 0)
                dve.wait_ge(below_ready, g + 1)
                seq.did(nc.vector.scalar_tensor_tensor(out=marks[:], in0=below[:], scalar=0.0,
                                                       in1=rank[:].unsqueeze(1).broadcast_to([128, TI, E]),
                                                       op0=ALU.is_equal, op1=ALU.mult))
                tiles(measure, 1)
                seq.wait(g)
                seq.did(nc.vector.reduce_max(best[:], marks[:], AX_X))
                tiles(measure, 2)
                seq.wait(g)
                after(dve, places_done, g - 1)
                seq.did(nc.vector.tensor_tensor(onehot[s][:], marks[:], bc(best), ALU.is_equal))
                nc.vector.tensor_scalar(first[:], best[:], -float(C), float(E * C), ALU.mult, ALU.add)
                tiles(measure, 3)
                seq.wait(g)
                seq.did(nc.vector.tensor_reduce(count[:], onehot[s][:].rearrange("p t e -> p e t"), AX_X, ALU.add))
                tiles(measure, 4)
                seq.wait(g)
                nc.vector.tensor_tensor(counted[1 - s][:], counted[s][:], count[:], ALU.add).then_inc(onehot_ready, 1)
                tiles(measure, 5, 6, 7)
                if ahead:
                    gather_statistics(g + 2)
                dve.wait_ge(exp_ready, g + 1)
                nc.vector.reduce_sum(total[:], expd[:], AX_X).then_inc(total_ready, 1)
                dve.wait_ge(places_done, g + 1)
                seq.did(nc.vector.tensor_tensor(picked[:], psC[s][:], onehot[s][:], ALU.mult))
                dve.wait_ge(total_ready, g + 1)
                after(dve, scattered[s], 16 * TI * i)
                nc.vector.reciprocal(entry[s][:, :, 1].bitcast(F32), total[:])
                nc.vector.tensor_copy(entry[s][:, :, 0], R.tokens[:, bass.ds(g * TI, TI)])
                seq.wait(g)
                seq.did(nc.vector.reduce_sum(place[:], picked[:], AX_X))
                if ahead:
                    inverse_deviation(g + 2)
                seq.wait(g)
                nc.vector.tensor_scalar(inside[:], place[:], float(C), None, ALU.is_lt)
                seq.did(nc.vector.tensor_tensor(spot[:], first[:], place[:], ALU.add))
                tiles(normalise, 0, 1)
                seq.wait(g)
                seq.did(nc.vector.tensor_scalar(target[:], inside[:], -NONE, NONE, ALU.mult, ALU.add))
                tiles(normalise, 2, 3)
                seq.wait(g)
                nc.vector.tensor_tensor(target_row[s][:], target[:], spot[:], ALU.add).then_inc(targets_ready, 1)
                tiles(normalise, 4, 5, 6, 7)
                seq.check()
            groups(dve, NG, group)

        @block.tensor
        def _(pe):
            pe.wait_ge(wg_loaded, 16)
            pe.wait_ge(set_up, 1)

            def transposes(g, s):
                pe.wait_ge(xn_ready, g + 1)
                after(pe, xT_ready, g)
                for t in range(TI):
                    for k in range(2):
                        last = nc.tensor.transpose(psT[:, k, 128 * t:128 * t + 128], XN[s][:, t, 128 * k:128 * k + 128], T.ident[:])
                last.then_inc(xT_done, 1)

            def logits(g, s):
                pe.wait_ge(xT_ready, g + 1)
                after(pe, below_ready, g - 1)
                for t in range(TI):
                    for k in range(2):
                        last = nc.tensor.matmul(psL[s][:, t, :], xT[s][:, k, 128 * t:128 * t + 128], wg[:, k, :],
                                                start=k == 0, stop=k == 1)
                last.then_inc(logits_done, 1)

            def places(g, s):
                pe.wait_ge(onehot_ready, g + 1)
                after(pe, targets_ready, g - 1)
                for t in range(TI):
                    nc.tensor.matmul(psC[s][:, t, :], earlier[:], onehot[s][:, t, :], start=True, stop=False)
                    for before in range(t):
                        nc.tensor.matmul(psC[s][:, t, :], ones[:], onehot[s][:, before, :], start=False, stop=False)
                    last = nc.tensor.matmul(psC[s][:, t, :], ones[:], counted[s][:], start=False, stop=True)
                last.then_inc(places_done, 1)
            transposes(0, 0)
            logits(0, 0)

            def group(g, s, i):
                if next_is_there(g):
                    transposes(g + 1, 1 - s)
                places(g, s)
                if next_is_there(g):
                    logits(g + 1, 1 - s)
            groups(pe, NG, group)


def expert_stage(nc, T, R, stage, x, table, w1, w2):
    N = x.shape[0]
    E, D, F = w1.shape
    C = R.C
    G = 512 if C % 1024 == 0 else C // 2
    TI = G // 128
    NG = E * C // G
    NF = F // 128
    with ExitStack() as ctx:
        sb, ps, sem = tools(nc, ctx, stage)
        slots = sb("slots", [128, NG, TI, 2], U32)
        index = [sb(f"index{q}", [128, TI], U32) for q in range(4)]
        gate = [sb(f"gate{q}", [128, TI], F32) for q in range(4)]
        XG = [sb(f"xg{q}", [128, TI, D], F32) for q in range(4)]
        XN = sb("xn", [128, TI, D], F32)
        stats = sb("stats", [128, TI, 6], F32)
        mv = sb("mv", [128, TI, 2], F32)
        std = sb("std", [128, TI], F32)
        rstd = sb("rstd", [128, TI], F32)
        xhi = [sb(f"xhi{s}", [128, 2, G], F32R) for s in range(2)]
        xlo = [sb(f"xlo{s}", [128, 2, G], F32R) for s in range(2)]
        w1_raw = sb("w1_raw", [128, 2, F], F32)
        w2_raw = sb("w2_raw", [128, NF, D], F32)
        w1_hi = [sb(f"w1_hi{s}", [128, 2, F], F32R) for s in range(2)]
        w1_lo = [sb(f"w1_lo{s}", [128, 2, F], F32R) for s in range(2)]
        w2_hi = [sb(f"w2_hi{s}", [128, NF, D], F32R) for s in range(2)]
        w2_lo = [sb(f"w2_lo{s}", [128, NF, D], F32R) for s in range(2)]
        h_hi = [sb(f"h_hi{s}", [128, G], F32R) for s in range(2)]
        h_lo = [sb(f"h_lo{s}", [128, G], F32R) for s in range(2)]
        Y = [sb(f"y{s}", [128, TI, D], F32) for s in range(2)]
        psT = ps("psT", [128, 2, 512])
        psH = [ps(f"psH{s}", [128, 512]) for s in range(2)]
        psE = [ps(f"psE{s}", [128, 4, D]) for s in range(2)]

        table_loaded = sem("table_loaded")
        w_loaded, w_ready, hi_written = sem("w_loaded"), sem("w_ready"), sem("w_hi_written")
        index_ready, gathered, scattered = sem("index_ready"), [sem(f"gathered{q}") for q in range(4)], [sem(f"scattered{s}") for s in range(2)]
        measured, stats_ready, std_ready, rstd_ready, xn_ready = sem("measured"), sem("stats_ready"), sem("std_ready"), sem("rstd_ready"), sem("xn_ready")
        xT_done, hi_ready, lo_ready = sem("xT_done"), sem("hi_ready"), sem("lo_ready")
        h_done, h_hi_ready, h_lo_ready = sem("h_done"), sem("h_hi_ready"), sem("h_lo_ready")
        h_used, y_ready, cleared = sem("h_used"), sem("y_ready"), sem("cleared")
        block = ctx.enter_context(nc.Block())

        def load_weights(sp, e):
            sp.dma_start(w1_raw[:], row(w1.rearrange("e (k p) f -> e p k f", p=128), e)).then_inc(w_loaded, 16)
            sp.dma_start(w2_raw[:], row(w2.rearrange("e (f p) d -> e p f d", p=128), e)).then_inc(w_loaded, 16)

        QUARTERS = [(w1_raw, w1_hi, w1_lo, 0), (w1_raw, w1_hi, w1_lo, 1), (w2_raw, w2_hi, w2_lo, 0), (w2_raw, w2_hi, w2_lo, 1)]

        def quarter(w, part):
            return w[:, part, :] if w.shape[1] == 2 else w[:, NF // 2 * part:NF // 2 * (part + 1), :]

        def next_is_there(g, n=1):
            return not (isinstance(g, int) and g + n >= NG)

        def all_groups(eng, body):
            def expert(e, ws, turn):
                body(e * 2, 0, e, ws, 2 * ws, turn)
                body(e * 2 + 1, 1, e, ws, 2 * ws + 1, turn)
            groups(eng, E, expert)

        @block.sync
        def _(sp):
            sp.dma_start(slots[:], table.rearrange("(g p t) o -> p g t o", t=TI, p=128)).then_inc(table_loaded, 16)
            load_weights(sp, 0)

            def group(g, s, e, ws, q, turn):
                if s == 0 and next_is_there(g, 2):
                    sp.wait_ge(w_ready, 4 * e + 4)
                    load_weights(sp, e + 1)
            all_groups(sp, group)

        @block.gpsimd
        def _(pool):
            def gather(g, q):
                if isinstance(g, int) and g < 4:
                    pool.wait_ge(cleared, g + 1)
                pool.wait_ge(index_ready, g + 1)
                after(pool, y_ready, g - 3)
                T.settle(pool)
                for t in range(TI):
                    nc.gpsimd.indirect_dma_start(XG[q][:, t, :], None, x, bass.IndirectOffsetOnAxis(ap=index[q][:, t:t + 1], axis=0),
                                                 bounds_check=N - 1, oob_is_err=False).then_inc(gathered[q], 16)

            def scatter(g, s, q):
                pool.wait_ge(y_ready, g + 1)
                T.settle(pool)
                for t in range(TI):
                    nc.gpsimd.indirect_dma_start(x, bass.IndirectOffsetOnAxis(ap=index[q][:, t:t + 1], axis=0), Y[s][:, t, :], None,
                                                 bounds_check=N - 1, oob_is_err=False).then_inc(scattered[s], 16)
            gather(0, 0)
            gather(1, 1)

            def group(g, s, e, ws, q, turn):
                if not (isinstance(g, int) and g == 0):
                    scatter(g - 1, 1 - s, (q + 3) % 4)
                if next_is_there(g, 2):
                    gather(g + 2, (q + 2) % 4)
            all_groups(pool, group)
            scatter(NG - 1, 1, (NG - 1) % 4)
            for s in range(2):
                pool.wait_ge(scattered[s], 16 * TI * (NG // 2))

        @block.scalar
        def _(act):
            def deviation(g):
                act.wait_ge(stats_ready, g + 1)
                nc.scalar.activation(std[:], mv[:, :, 1], ACT.Sqrt, bias=T.eps[:]).then_inc(std_ready, 1)

            def split_x_hi(g, s):
                act.wait_ge(xT_done, g + 1)
                after(act, h_done, NF * (g - 1))
                nc.scalar.activation(xhi[s][:], psT[:, :, 0:G], ACT.Copy).then_inc(hi_ready, 1)

            def split_w_hi(s, e, c):
                if c == 0:
                    act.wait_ge(w_loaded, 32 * e + 32)
                    after(act, h_used, NF * (2 * e - 2))
                raw, hi, _, part = QUARTERS[c]
                nc.scalar.activation(quarter(hi[s], part), quarter(raw, part), ACT.Copy).then_inc(hi_written, 1)

            deviation(0)
            for c in range(2):
                split_w_hi(0, 0, c)
            split_x_hi(0, 0)
            for c in range(2, 4):
                split_w_hi(0, 0, c)

            def group(g, s, e, ws, q, turn):
                for f in range(NF):
                    act.wait_ge(h_done, NF * g + f + 1)
                    after(act, h_used, NF * g + f - 1)
                    nc.scalar.activation(h_hi[f % 2][:], psH[f % 2][:, 0:G], ACT.Relu).then_inc(h_hi_ready, 1)
                    if s == 1 and f in (1, 3, 4, 6) and next_is_there(g):
                        split_w_hi(1 - ws, e + 1, (1, 3, 4, 6).index(f))
                    if f == 2 and next_is_there(g):
                        deviation(g + 1)
                    if f == 5 and next_is_there(g):
                        split_x_hi(g + 1, 1 - s)
            all_groups(act, group)

        @block.vector
        def _(dve):
            def fetch_slots(g, q):
                nc.vector.tensor_copy(index[q][:], slots[:, bass.ds(g, 1), :, 0].rearrange("p o t -> p (o t)"))
                nc.vector.tensor_copy(gate[q][:], slots[:, bass.ds(g, 1), :, 1].rearrange("p o t -> p (o t)").bitcast(F32)).then_inc(index_ready, 1)

            def measure(g, q, turn):
                dve.wait_ge(gathered[q], 16 * TI * (turn + 1))
                for t in range(TI):
                    last = nc.vector.bn_stats(stats[:, t, :], XG[q][:, t, :])
                last.then_inc(measured, 1)

            def gather_statistics(g):
                dve.wait_ge(measured, g + 1)
                after(dve, std_ready, g)
                T.settle(dve)
                for t in range(TI):
                    last = nc.vector.bn_aggr(mv[:, t, :], stats[:, t, :])
                last.then_inc(stats_ready, 1)

            def normalise(g, q):
                dve.wait_ge(std_ready, g + 1)
                nc.vector.reciprocal(rstd[:], std[:]).then_inc(rstd_ready, 1)
                dve.wait_ge(rstd_ready, g + 1)
                after(dve, xT_done, g)
                for t in range(TI):
                    last = nc.vector.tensor_scalar(XN[:, t, :], XG[q][:, t, :], mv[:, t, 0:1], rstd[:, t:t + 1], ALU.subtract, ALU.mult)
                last.then_inc(xn_ready, 1)

            def split_x_lo(g, s):
                dve.wait_ge(hi_ready, g + 1)
                nc.vector.tensor_tensor(xlo[s][:], psT[:, :, 0:G], xhi[s][:].bitcast(F32), ALU.subtract).then_inc(lo_ready, 1)

            def split_w_lo(s, e, c):
                dve.wait_ge(hi_written, 4 * e + c + 1)
                raw, hi, lo, part = QUARTERS[c]
                nc.vector.tensor_tensor(quarter(lo[s], part), quarter(raw, part), quarter(hi[s], part).bitcast(F32),
                                        ALU.subtract).then_inc(w_ready, 1)

            def add_outputs(g, s, e, q):
                dve.wait_ge(h_used, NF * g + NF)
                after(dve, scattered[s], 16 * TI * e)
                for t in range(TI):
                    last = nc.vector.scalar_tensor_tensor(out=Y[s][:, t, :], in0=psE[s][:, t, :], scalar=gate[q][:, t:t + 1],
                                                          in1=XG[q][:, t, :], op0=ALU.mult, op1=ALU.add)
                last.then_inc(y_ready, 1)

            for q in range(4):
                nc.vector.memset(XG[q][:], 0.0).then_inc(cleared, 1)
            dve.wait_ge(table_loaded, 16)
            for g in range(2):
                fetch_slots(g, g)
            measure(0, 0, 0)
            gather_statistics(0)
            normalise(0, 0)
            for c in range(2):
                split_w_lo(0, 0, c)
            split_x_lo(0, 0)
            for c in range(2, 4):
                split_w_lo(0, 0, c)

            def group(g, s, e, ws, q, turn):
                for f in range(NF):
                    dve.wait_ge(h_hi_ready, NF * g + f + 1)
                    nc.vector.scalar_tensor_tensor(out=h_lo[f % 2][:], in0=psH[f % 2][:, 0:G], scalar=0.0,
                                                   in1=h_hi[f % 2][:].bitcast(F32), op0=ALU.max, op1=ALU.subtract).then_inc(h_lo_ready, 1)
                    if f == 0:
                        if next_is_there(g, 2):
                            after(dve, scattered[s], 16 * TI * e)
                            fetch_slots(g + 2, (q + 2) % 4)
                        if not (isinstance(g, int) and g == 0):
                            add_outputs(g - 1, 1 - s, e if s == 1 else e - 1, (q + 3) % 4)
                    if f == 1 and next_is_there(g):
                        measure(g + 1, (q + 1) % 4, turn + 1 if q == 3 else turn)
                    if f == 2 and next_is_there(g):
                        gather_statistics(g + 1)
                    if f == 3 and next_is_there(g):
                        normalise(g + 1, (q + 1) % 4)
                    if s == 1 and f in (2, 4, 6, 7) and next_is_there(g):
                        split_w_lo(1 - ws, e + 1, (2, 4, 6, 7).index(f))
                    if f == 5 and next_is_there(g):
                        split_x_lo(g + 1, 1 - s)
            all_groups(dve, group)
            add_outputs(NG - 1, 1, E - 1, (NG - 1) % 4)

        @block.tensor
        def _(pe):
            def transposes(g):
                pe.wait_ge(xn_ready, g + 1)
                after(pe, lo_ready, g)
                for t in range(TI):
                    for k in range(2):
                        last = nc.tensor.transpose(psT[:, k, 128 * t:128 * t + 128], XN[:, t, 128 * k:128 * k + 128], T.ident[:])
                last.then_inc(xT_done, 1)

            def up(g, s, e, ws, f):
                if f == 0:
                    pe.wait_ge(lo_ready, g + 1)
                    if s == 0:
                        pe.wait_ge(w_ready, 4 * e + 2)
                after(pe, h_lo_ready, NF * g + f - 1)
                fs = slice(128 * f, 128 * f + 128)
                three_pass(nc, psH[f % 2][:, 0:G], [(w1_hi[ws][:, k, fs], w1_lo[ws][:, k, fs], xhi[s][:, k, :], xlo[s][:, k, :])
                                                    for k in range(2)]).then_inc(h_done, 1)

            def down(g, s, e, ws, f):
                pe.wait_ge(h_lo_ready, NF * g + f + 1)
                if f == 0:
                    after(pe, y_ready, g - 1)
                    if s == 0:
                        pe.wait_ge(w_ready, 4 * e + 4)
                for t in range(TI):
                    tok = slice(128 * t, 128 * t + 128)
                    last = three_pass(nc, psE[s][:, t, :], [(h_hi[f % 2][:, tok], h_lo[f % 2][:, tok], w2_hi[ws][:, f, :], w2_lo[ws][:, f, :])],
                                      start=f == 0 and t % 2 == 0, stop=f == NF - 1, skip_group_check=True)
                last.then_inc(h_used, 1)

            transposes(0)
            up(0, 0, 0, 0, 0)

            def group(g, s, e, ws, q, turn):
                for f in range(NF):
                    if f + 1 < NF:
                        up(g, s, e, ws, f + 1)
                    elif next_is_there(g):
                        up(g + 1, 1 - s, e + s, ws if s == 0 else 1 - ws, 0)
                    if f == 4 and next_is_there(g):
                        transposes(g + 1)
                    down(g, s, e, ws, f)
            all_groups(pe, group)


def projection_stage(nc, T, stage, x, wT, qk, v):
    N, D = x.shape
    G = 512
    NG = N // G
    H, HD = 16, 16
    xg_ = x.rearrange("(g t p) d -> g p t d", t=4, p=128)
    qkb = qk.rearrange("r (b h) d n -> b r (h d) n", h=H)
    vb = v.rearrange("(b h) p k w -> b p h k w", h=H)
    with ExitStack() as ctx:
        sb, ps, sem = tools(nc, ctx, stage)
        X = [sb(f"x{s}", [128, 4, D], F32) for s in range(2)]
        XN = [sb(f"xn{s}", [128, 4, D], F32) for s in range(2)]
        xhi = [sb(f"xhi{s}", [128, 2, G], F32R) for s in range(2)]
        xlo = [sb(f"xlo{s}", [128, 2, G], F32R) for s in range(2)]
        QKH = [sb(f"qkh{s}", [128, 4, G], F32R) for s in range(2)]
        QKL = [sb(f"qkl{s}", [128, 4, G], F32R) for s in range(2)]
        VA = [sb(f"va{s}", [128, H, 4, 32], F32) for s in range(2)]
        stats = sb("stats", [128, 4, 6], F32)
        mv = sb("mv", [128, 4, 2], F32)
        std = sb("std", [128, 4], F32)
        rstd = sb("rstd", [128, 4], F32)
        w_raw = sb("w_raw", [128, 2, 3 * D], F32)
        w_hi = sb("w_hi", [128, 2, 3 * D], F32R)
        w_lo = sb("w_lo", [128, 2, 3 * D], F32R)
        psT = ps("psT", [128, 2, G])
        psQ = [ps(f"psQ{s}", [128, G]) for s in range(2)]
        psV = [ps(f"psV{s}", [128, 2, D]) for s in range(2)]

        w_loaded, w_hi_ready, w_ready, set_up = sem("w_loaded"), sem("w_hi_ready"), sem("w_ready"), sem("set_up")
        x_loaded, qkv_stored = [sem(f"x_loaded{s}") for s in range(2)], [sem(f"qkv_stored{s}") for s in range(2)]
        stats_ready, std_ready, xn_ready = sem("stats_ready"), sem("std_ready"), sem("xn_ready")
        xT_done, hi_ready, lo_ready = sem("xT_done"), sem("hi_ready"), sem("lo_ready")
        qk_done, qk_hi_ready, qk_lo_ready, v_done, v_ready = sem("qk_done"), sem("qk_hi_ready"), sem("qk_lo_ready"), sem("v_done"), sem("v_ready")
        measured, rstd_ready = sem("measured"), sem("rstd_ready")
        block = ctx.enter_context(nc.Block())

        def next_is_there(g, n=1):
            return not (isinstance(g, int) and g + n >= NG)

        @block.sync
        def _(sp):
            sp.dma_start(w_raw[:], wT.rearrange("(k p) n -> p k n", p=128)).then_inc(w_loaded, 16)
            for g in range(2):
                sp.dma_start(X[g][:], xg_[g]).then_inc(x_loaded[g], 16)

            def store_qkv(g, s, i):
                half = slice(G * s, G * s + G)
                sp.wait_ge(qk_lo_ready, 4 * g + 4)
                for part in range(2):
                    cs = slice(2 * part, 2 * part + 2)
                    for r, buf in ((2 * part, QKH), (2 * part + 1, QKL)):
                        sp.dma_start(row(qkb, i)[r, :, half].rearrange("(c p) n -> p c n", p=128), buf[s][:, cs, :].bitcast(F32)).then_inc(qkv_stored[s], 16)
                sp.wait_ge(v_ready, 2 * g + 2)
                sp.dma_start(row(vb, i)[:, :, 4 * s:4 * s + 4, :], VA[s][:]).then_inc(qkv_stored[s], 16)

            def group(g, s, i):
                if next_is_there(g, 2):
                    sp.wait_ge(xn_ready, g + 1)
                    sp.dma_start(X[s][:], row(xg_, g + 2)).then_inc(x_loaded[s], 16)
                if not (isinstance(g, int) and g == 0):
                    store_qkv(g - 1, 1 - s, i if s == 1 else i - 1)
            groups(sp, NG, group)
            store_qkv(NG - 1, 1, NG // 2 - 1)
            for s in range(2):
                sp.wait_ge(qkv_stored[s], 80 * (NG // 2))

        @block.gpsimd
        def _(pool):
            for s in range(2):
                nc.gpsimd.memset(VA[s][:], 0.0).then_inc(set_up, 1)
            pool.wait_ge(set_up, 2)
            for s in range(2):
                nc.gpsimd.memset(VA[s][:, :, :, HD:HD + 1], 1.0).then_inc(set_up, 1)

        @block.scalar
        def _(act):
            act.wait_ge(set_up, 4)

            def deviation(g):
                act.wait_ge(stats_ready, g + 1)
                nc.scalar.activation(std[:], mv[:, :, 1], ACT.Sqrt, bias=T.eps[:]).then_inc(std_ready, 1)

            def split_hi(g, s):
                act.wait_ge(xT_done, g + 1)
                after(act, v_done, 2 * g - 2)
                nc.scalar.activation(xhi[s][:], psT[:], ACT.Copy).then_inc(hi_ready, 1)
            deviation(0)
            split_hi(0, 0)
            deviation(1)

            def group(g, s, i):
                after(act, qkv_stored[s], 80 * i)
                for c in range(4):
                    act.wait_ge(qk_done, 4 * g + c + 1)
                    nc.scalar.activation(QKH[s][:, c, :], psQ[c % 2][:], ACT.Copy, scale=D ** -0.5).then_inc(qk_hi_ready, 1)
                    if c == 2 and next_is_there(g):
                        split_hi(g + 1, 1 - s)
                for c in range(2):
                    act.wait_ge(v_done, 2 * g + c + 1)
                    nc.scalar.activation(VA[s][:, :, 2 * c:2 * c + 2, 0:HD].rearrange("p h t d -> p t h d"),
                                         psV[c][:].rearrange("p t (h d) -> p t h d", h=H), ACT.Copy, scale=D ** -0.5).then_inc(v_ready, 1)
                if next_is_there(g, 2):
                    deviation(g + 2)
            groups(act, NG, group)

        @block.vector
        def _(dve):
            dve.wait_ge(w_loaded, 16)
            nc.vector.tensor_copy(w_hi[:], w_raw[:]).then_inc(w_hi_ready, 1)
            dve.wait_ge(w_hi_ready, 1)
            nc.vector.tensor_tensor(w_lo[:], w_raw[:], w_hi[:].bitcast(F32), ALU.subtract).then_inc(w_ready, 1)

            def measure(g, s, i):
                dve.wait_ge(x_loaded[s], 16 * (i + 1))
                for t in range(4):
                    last = nc.vector.bn_stats(stats[:, t, :], X[s][:, t, :])
                last.then_inc(measured, 1)

            def gather_statistics(g):
                dve.wait_ge(measured, g + 1)
                after(dve, std_ready, g)
                T.settle(dve)
                for t in range(4):
                    last = nc.vector.bn_aggr(mv[:, t, :], stats[:, t, :])
                last.then_inc(stats_ready, 1)

            def normalise(g, s):
                dve.wait_ge(std_ready, g + 1)
                nc.vector.reciprocal(rstd[:], std[:]).then_inc(rstd_ready, 1)
                dve.wait_ge(rstd_ready, g + 1)
                after(dve, xT_done, g - 1)
                for t in range(4):
                    last = nc.vector.tensor_scalar(XN[s][:, t, :], X[s][:, t, :], mv[:, t, 0:1], rstd[:, t:t + 1],
                                                   ALU.subtract, ALU.mult)
                last.then_inc(xn_ready, 1)

            def split_lo(g, s):
                dve.wait_ge(hi_ready, g + 1)
                nc.vector.tensor_tensor(xlo[s][:], psT[:], xhi[s][:].bitcast(F32), ALU.subtract).then_inc(lo_ready, 1)

            for g in range(2):
                measure(g, g, 0)
                if g == 1:
                    split_lo(0, 0)
                gather_statistics(g)
                if g == 0:
                    normalise(0, 0)

            def group(g, s, i):
                for c in range(4):
                    dve.wait_ge(qk_hi_ready, 4 * g + c + 1)
                    nc.vector.scalar_tensor_tensor(out=QKL[s][:, c, :], in0=psQ[c % 2][:], scalar=D ** -0.5,
                                                   in1=QKH[s][:, c, :].bitcast(F32), op0=ALU.mult, op1=ALU.subtract).then_inc(qk_lo_ready, 1)
                    if c == 0 and next_is_there(g):
                        normalise(g + 1, 1 - s)
                    if c == 2:
                        if next_is_there(g, 2):
                            measure(g + 2, s, i + 1)
                        if next_is_there(g):
                            split_lo(g + 1, 1 - s)
                    if c == 3 and next_is_there(g, 2):
                        gather_statistics(g + 2)
            groups(dve, NG, group)

        @block.tensor
        def _(pe):
            pe.wait_ge(w_ready, 1)

            def transposes(g, s):
                pe.wait_ge(xn_ready, g + 1)
                after(pe, lo_ready, g)
                for t in range(4):
                    for k in range(2):
                        last = nc.tensor.transpose(psT[:, k, 128 * t:128 * t + 128], XN[s][:, t, 128 * k:128 * k + 128], T.ident[:])
                last.then_inc(xT_done, 1)
            transposes(0, 0)

            def group(g, s, i):
                pe.wait_ge(lo_ready, g + 1)
                for c in range(4):
                    after(pe, qk_lo_ready, 4 * g + c - 1)
                    three_pass(nc, psQ[c % 2][:], [(w_hi[:, k, 128 * c:128 * c + 128], w_lo[:, k, 128 * c:128 * c + 128],
                                                    xhi[s][:, k, :], xlo[s][:, k, :]) for k in range(2)]).then_inc(qk_done, 1)
                    if c == 2 and next_is_there(g):
                        transposes(g + 1, 1 - s)
                for c in range(2):
                    after(pe, v_ready, 2 * g + c - 1)
                    for t in range(2):
                        tok = slice(256 * c + 128 * t, 256 * c + 128 * t + 128)
                        last = three_pass(nc, psV[c][:, t, :], [(xhi[s][:, k, tok], xlo[s][:, k, tok], w_hi[:, k, 2 * D:], w_lo[:, k, 2 * D:])
                                                                for k in range(2)])
                    last.then_inc(v_done, 1)
            groups(pe, NG, group)


def attention_stage(nc, T, stage, x, qk, v, woT, out):
    N, D = x.shape
    S = 1024
    B = N // S
    H, HD = 16, 16
    NH = B * H
    KC = S // 128
    MROW = 96
    OUT_SCALE = S / float(S - 1) ** 0.5 * S ** -0.5 * D ** -0.5
    xb = x.rearrange("(b t p) d -> b p t d", t=KC, p=128)
    ob = out.rearrange("(b t p) d -> b p t d", t=KC, p=128)
    qkh = qk.rearrange("r h d n -> h r d n")
    with ExitStack() as ctx:
        sb, ps, sem = tools(nc, ctx, stage)
        Q = [sb(f"q{j}", [MROW + 2, S], F32R) for j in range(4)]
        K = [sb(f"k{j}", [MROW + 2, S], F32R) for j in range(4)]
        V = [sb(f"v{j}", [128, KC, 32], F32) for j in range(4)]
        P = [sb(f"p{j}", [128, S], F32) for j in range(4)]
        best = [sb(f"best{j}", [128, KC, 2], F32) for j in range(2)]
        mx = [sb(f"mx{j}", [128, KC], F32) for j in range(2)]
        nm_hi = [sb(f"nm_hi{j}", [KC, 128], F32R) for j in range(2)]
        nm_lo = [sb(f"nm_lo{j}", [KC, 128], F32R) for j in range(2)]
        OT = sb("oT", [128, 256], F32)
        rden = sb("rden", [128, 2, 4], F32)
        O = sb("o", [128, KC, D], F32)
        oT_hi = sb("oT_hi", [128, 2, S], F32R)
        oT_lo = sb("oT_lo", [128, 2, S], F32R)
        X = sb("x", [128, KC, D], F32)
        Y = sb("y", [128, KC, D], F32)
        w_raw = sb("w_raw", [128, 2, D], F32)
        w_hi = sb("w_hi", [128, 2, D], F32R)
        w_lo = sb("w_lo", [128, 2, D], F32R)
        psM = [ps(f"psM{s}", [128, 512]) for s in range(2)]
        psE = [ps(f"psE{s}", [128, 2, 512]) for s in range(2)]
        psO = ps("psO", [128, 512])
        psX = ps("psX", [128, 512])

        w_loaded, w_hi_ready, w_ready, set_up, zeroed = sem("w_loaded"), sem("w_hi_ready"), sem("w_ready"), sem("set_up"), sem("zeroed")
        qkv_loaded = [sem(f"qkv_loaded{j}") for j in range(4)]
        max_loaded = [sem(f"max_loaded{j}") for j in range(4)]
        x_loaded, y_stored = sem("x_loaded"), sem("y_stored")
        m_done, m_taken, mx_ready = sem("m_done"), sem("m_taken"), sem("mx_ready")
        mT_done, nm_hi_ready, nm_lo_ready = sem("mT_done"), sem("nm_hi_ready"), sem("nm_lo_ready")
        e_done, p_ready, pv_done = sem("e_done"), sem("p_ready"), sem("pv_done")
        oT_ready, t_done, o_ready, rden_ready = sem("oT_ready"), sem("t_done"), sem("o_ready"), sem("rden_ready")
        xo_done, xo_hi_ready, xo_lo_ready, wo_done, y_ready = sem("xo_done"), sem("xo_hi_ready"), sem("xo_lo_ready"), sem("wo_done"), sem("y_ready")
        block = ctx.enter_context(nc.Block())

        def heads(eng, step, batch_end):
            def batch(b, last):
                first = b * 4
                step(first * 4, 0, first, 0)
                if not (isinstance(b, int) and b == 0):
                    batch_end(b - 1)
                for j in range(1, 4):
                    step(first * 4 + j, j, first, j)
                with eng.Fori(1, 3 if last else 4) as q:
                    for j in range(4):
                        step((first + q) * 4 + j, j, first + q, q * 4 + j)
                if last:
                    for j in range(4):
                        step(first * 4 + 12 + j, j, first + 3, 12 + j)
            batch(0, B == 1)
            if B > 2:
                batch(1, False)
            if B > 3:
                with eng.Fori(2, B - 1) as b:
                    batch(b, False)
            if B > 1:
                batch(B - 1, True)

        @block.sync
        def _(sp):
            def load_head(hh, j):
                sp.dma_start(Q[j][0:32, :].bitcast(F32), row(qkh, hh)[0:2]).then_inc(qkv_loaded[j], 16)
                sp.dma_start(Q[j][32:48, :].bitcast(F32), row(qkh, hh)[0]).then_inc(qkv_loaded[j], 16)
                sp.dma_start(K[j][0:16, :].bitcast(F32), row(qkh, hh)[2]).then_inc(qkv_loaded[j], 16)
                sp.dma_start(K[j][16:48, :].bitcast(F32), row(qkh, hh)[2:4]).then_inc(qkv_loaded[j], 16)
                sp.dma_start(V[j][:], row(v, hh)).then_inc(qkv_loaded[j], 16)

            def load_max(hh, j):
                sp.wait_ge(nm_lo_ready, hh + 1)
                sp.dma_start(Q[j][MROW:MROW + 1, :].bitcast(F32), nm_hi[j % 2][:].bitcast(F32)).then_inc(max_loaded[j], 16)
                sp.dma_start(Q[j][MROW + 1:MROW + 2, :].bitcast(F32), nm_lo[j % 2][:].bitcast(F32)).then_inc(max_loaded[j], 16)

            sp.dma_start(w_raw[:], woT.rearrange("(k p) n -> p k n", p=128)).then_inc(w_loaded, 16)
            sp.dma_start(X[:], xb[0]).then_inc(x_loaded, 16)
            sp.wait_ge(set_up, 1)
            for h in range(3):
                load_head(h, h)
            load_max(0, 0)

            def step(hh, j, turn, h):
                if not (isinstance(hh, int) and hh + 3 >= NH):
                    after(sp, e_done, hh * KC)
                    after(sp, pv_done, hh * KC)
                    load_head(hh + 3, (j + 3) % 4)
                if not (isinstance(hh, int) and hh + 1 >= NH):
                    load_max(hh + 1, (j + 1) % 4)

            def batch_end(b):
                sp.wait_ge(y_ready, 4 * b + 4)
                sp.dma_start(row(ob, b), Y[:]).then_inc(y_stored, 16)
                if not (isinstance(b, int) and b + 1 >= B):
                    sp.dma_start(X[:], row(xb, b + 1)).then_inc(x_loaded, 16)
            heads(sp, step, batch_end)
            batch_end(B - 1)
            sp.wait_ge(y_stored, 16 * B)

        @block.gpsimd
        def _(pool):
            for j in range(4):
                nc.gpsimd.memset(Q[j][:].bitcast(F32), 0.0)
                last = nc.gpsimd.memset(K[j][:].bitcast(F32), 0.0)
            last.then_inc(zeroed, 1)
            pool.wait_ge(zeroed, 1)
            for j in range(4):
                last = nc.gpsimd.memset(K[j][MROW:MROW + 2, :].bitcast(F32), 1.0)
            last.then_inc(set_up, 1)

        @block.scalar
        def _(act):
            act.wait_ge(w_loaded, 16)
            nc.scalar.activation(w_hi[:], w_raw[:], ACT.Copy).then_inc(w_hi_ready, 1)

            def take_max(hh, j, turn):
                act.wait_ge(mT_done, hh + 1)
                after(act, max_loaded[(j + 2) % 4], (turn + 1 if j >= 2 else turn) * 32)
                nc.scalar.activation(nm_hi[j % 2][:], psX[0:KC, 256:384], ACT.Copy, scale=-1.0).then_inc(nm_hi_ready, 1)

            def exps(hh, kc):
                act.wait_ge(e_done, hh * KC + kc + 1)
                after(act, pv_done, hh * KC + kc - 3)
                nc.scalar.activation(P[kc % 4][:], psE[kc % 2][:].rearrange("p a b -> p (a b)"), ACT.Exp, scale=HD ** -0.5).then_inc(p_ready, 1)

            def take_values(hh):
                act.wait_ge(pv_done, hh * KC + KC)
                after(act, t_done, hh)
                nc.scalar.activation(OT[:], psO[:, 0:256], ACT.Copy).then_inc(oT_ready, 1)

            take_max(0, 0, 0)

            def step(hh, j, turn, h):
                for kc in range(KC):
                    exps(hh, kc)
                    if kc == 1 and not (isinstance(hh, int) and hh == 0):
                        take_values(hh - 1)
                    if kc == 0 and not (isinstance(hh, int) and hh + 1 >= NH):
                        take_max(hh + 1, (j + 1) % 4, turn if j < 3 else turn + 1)

            def batch_end(b):
                for half in range(2):
                    for k in range(2):
                        act.wait_ge(xo_done, 4 * b + 2 * half + k + 1)
                        nc.scalar.activation(oT_hi[:, k, 512 * half:512 * half + 512], psE[half][:, k, :], ACT.Copy).then_inc(xo_hi_ready, 1)
            heads(act, step, batch_end)
            take_values(NH - 1)
            batch_end(B - 1)

        @block.vector
        def _(dve):
            dve.wait_ge(w_hi_ready, 1)
            nc.vector.tensor_tensor(w_lo[:], w_raw[:], w_hi[:].bitcast(F32), ALU.subtract).then_inc(w_ready, 1)

            def maximum(hh, qt, j):
                for half in range(2):
                    dve.wait_ge(m_done, hh * (2 * KC) + 2 * qt + half + 1)
                    nc.vector.reduce_max(best[j % 2][:, qt, half:half + 1], psM[half][:], AX_X).then_inc(m_taken, 1)

            def whole_maximum(hh, j):
                dve.wait_ge(m_taken, hh * (2 * KC) + 2 * KC)
                after(dve, mT_done, hh - 1)
                nc.vector.tensor_tensor(mx[j % 2][:], best[j % 2][:, :, 0], best[j % 2][:, :, 1], ALU.max).then_inc(mx_ready, 1)

            def max_lo(hh, j):
                dve.wait_ge(nm_hi_ready, hh + 1)
                nc.vector.scalar_tensor_tensor(out=nm_lo[j % 2][:], in0=psX[0:KC, 256:384], scalar=-1.0, in1=nm_hi[j % 2][:].bitcast(F32),
                                               op0=ALU.mult, op1=ALU.subtract).then_inc(nm_lo_ready, 1)

            def normalise(hh, h):
                dve.wait_ge(t_done, hh + 1)
                tv = psX[:, 0:256].rearrange("p (c j w) -> p c j w", c=2, j=4)
                nc.vector.reciprocal(rden[:], tv[:, :, :, HD]).then_inc(rden_ready, 1)
                dve.wait_ge(rden_ready, hh + 1)
                cols = O[:, :, bass.ds(h * HD, HD)].rearrange("p (j c) d -> p c j d", c=2)
                nc.vector.tensor_tensor(cols, tv[:, :, :, 0:HD], rden[:].unsqueeze(3).broadcast_to([128, 2, 4, HD]), ALU.mult).then_inc(o_ready, 1)

            for hh in range(2):
                for qt in range(KC):
                    maximum(hh, qt, hh)
                whole_maximum(hh, hh)
                if hh == 0:
                    max_lo(0, 0)

            def step(hh, j, turn, h):
                for qt in range(KC):
                    if not (isinstance(hh, int) and hh + 2 >= NH):
                        maximum(hh + 2, qt, j)
                    if qt == 2 and not (isinstance(hh, int) and hh + 1 >= NH):
                        max_lo(hh + 1, (j + 1) % 4)
                    if qt == 4 and not (isinstance(hh, int) and hh == 0):
                        normalise(hh - 1, (h - 1) % H if isinstance(h, int) else h - 1)
                if not (isinstance(hh, int) and hh + 2 >= NH):
                    whole_maximum(hh + 2, j)

            def batch_end(b):
                for half in range(2):
                    for k in range(2):
                        span = slice(512 * half, 512 * half + 512)
                        dve.wait_ge(xo_hi_ready, 4 * b + 2 * half + k + 1)
                        nc.vector.tensor_tensor(oT_lo[:, k, span], psE[half][:, k, :], oT_hi[:, k, span].bitcast(F32), ALU.subtract).then_inc(xo_lo_ready, 1)
                dve.wait_ge(x_loaded, (b + 1) * 16)
                after(dve, y_stored, b * 16)
                for quarter in range(4):
                    dve.wait_ge(wo_done, 4 * b + quarter + 1)
                    rows = slice(2 * quarter, 2 * quarter + 2)
                    nc.vector.scalar_tensor_tensor(out=Y[:, rows, :], in0=psM[quarter % 2][:].rearrange("p (t d) -> p t d", t=2), scalar=OUT_SCALE,
                                                   in1=X[:, rows, :], op0=ALU.mult, op1=ALU.add).then_inc(y_ready, 1)
            heads(dve, step, batch_end)
            normalise(NH - 1, H - 1)
            batch_end(B - 1)

        @block.tensor
        def _(pe):
            pe.wait_ge(set_up, 1)

            def scores_by_query(hh, qt, half, j, turn):
                if qt == 0 and half == 0:
                    pe.wait_ge(qkv_loaded[j], (turn + 1) * 80)
                after(pe, m_taken, hh * (2 * KC) + 2 * qt + half - 1)
                nc.tensor.matmul(psM[half][:], Q[j][0:MROW, 128 * qt:128 * qt + 128], K[j][0:MROW, 512 * half:512 * half + 512],
                                 start=True, stop=True).then_inc(m_done, 1)

            def max_rows(hh, j):
                pe.wait_ge(mx_ready, hh + 1)
                after(pe, o_ready, hh - 2)
                nc.tensor.transpose(psX[0:KC, 256:384], mx[j % 2][:], T.ident[:]).then_inc(mT_done, 1)

            def scores_by_key(hh, kc, j, turn):
                if kc == 0:
                    pe.wait_ge(max_loaded[j], (turn + 1) * 32)
                after(pe, p_ready, hh * KC + kc - 1)
                for half in range(2):
                    last = nc.tensor.matmul(psE[kc % 2][:, half, :], K[j][:, 128 * kc:128 * kc + 128], Q[j][:, 512 * half:512 * half + 512],
                                            start=True, stop=True)
                last.then_inc(e_done, 1)

            def values(hh, kc, j):
                pe.wait_ge(p_ready, hh * KC + kc + 1)
                if kc == 0:
                    after(pe, oT_ready, hh)
                for quarter in range(4):
                    last = nc.tensor.matmul(psO[32 * quarter:32 * quarter + 32, 0:256], V[j][:, kc, :], P[kc % 4][:, 256 * quarter:256 * quarter + 256],
                                            start=kc == 0, stop=kc == KC - 1)
                last.then_inc(pv_done, 1)

            def turn_values(hh):
                pe.wait_ge(oT_ready, hh + 1)
                if not (isinstance(hh, int) and hh + 2 >= NH):
                    pe.wait_ge(nm_lo_ready, hh + 3)
                after(pe, o_ready, hh)
                for c in range(2):
                    last = nc.tensor.transpose(psX[:, 128 * c:128 * c + 128], OT[:, 128 * c:128 * c + 128], T.ident[:])
                last.then_inc(t_done, 1)

            for hh in range(2):
                for qt in range(KC):
                    for half in range(2):
                        scores_by_query(hh, qt, half, hh, 0)
                if hh == 0:
                    max_rows(0, 0)

            def step(hh, j, turn, h):
                for kc in range(KC):
                    ahead = not (isinstance(hh, int) and hh + 2 >= NH)
                    if ahead:
                        scores_by_query(hh + 2, kc, 0, (j + 2) % 4, turn if j < 2 else turn + 1)
                    scores_by_key(hh, kc, j, turn)
                    if ahead:
                        scores_by_query(hh + 2, kc, 1, (j + 2) % 4, turn if j < 2 else turn + 1)
                    if kc >= 2:
                        values(hh, kc - 2, j)
                    elif not (isinstance(hh, int) and hh == 0):
                        values(hh - 1, KC - 2 + kc, (j + 3) % 4)
                    if kc == 0 and not (isinstance(hh, int) and hh + 1 >= NH):
                        max_rows(hh + 1, (j + 1) % 4)
                    if kc == 3 and not (isinstance(hh, int) and hh == 0):
                        turn_values(hh - 1)

            def batch_end(b):
                pe.wait_ge(o_ready, (b + 1) * H)
                pe.wait_ge(p_ready, (b + 1) * (H * KC) + (KC if not (isinstance(b, int) and b == B - 1) else 0))
                for half in range(2):
                    for k in range(2):
                        for t in range(4):
                            last = nc.tensor.transpose(psE[half][:, k, 128 * t:128 * t + 128], O[:, 4 * half + t, 128 * k:128 * k + 128], T.ident[:])
                        last.then_inc(xo_done, 1)
                pe.wait_ge(m_taken, (b + 1) * (H * 2 * KC) + (0 if isinstance(b, int) and b == B - 1 else 3 * 2 * KC))
                for quarter in range(4):
                    pe.wait_ge(xo_lo_ready, 4 * b + 2 * (quarter // 2) + 2)
                    if quarter == 0:
                        pe.wait_ge(w_ready, 1)
                    if quarter >= 2:
                        pe.wait_ge(y_ready, 4 * b + quarter - 1)
                    for t in range(2):
                        tok = slice(256 * quarter + 128 * t, 256 * quarter + 128 * t + 128)
                        last = three_pass(nc, psM[quarter % 2][:, 256 * t:256 * t + 256],
                                          [(oT_hi[:, k, tok], oT_lo[:, k, tok], w_hi[:, k, :], w_lo[:, k, :]) for k in range(2)])
                    last.then_inc(wo_done, 1)
                pe.wait_ge(y_ready, 4 * b + 4)
            heads(pe, step, batch_end)
            values(NH - 1, KC - 2, 3)
            values(NH - 1, KC - 1, 3)
            turn_values(NH - 1)
            batch_end(B - 1)


def hybrid_kernel(nc, x, wqkv_aT, bqkv_a, wqkv_bT, woT, wg, w1, w2, out):
    N, D = x.shape
    H, S = 16, 1024
    NH = N // S * H
    def scratch(name, shape, dt=F32):
        return nc.dram_tensor(f"scratch_{name}", shape, dt, kind="Internal").ap()
    att, x1 = scratch("att", [N, D]), scratch("x1", [N, D])
    qk, v = scratch("qk", [4, NH, 16, S]), scratch("v", [NH, 128, S // 128, 32])
    with ExitStack() as ctx:
        T = Shared(nc, ctx)
        R = Router(nc, ctx, N)
        table = scratch("table", [R.E * R.C, 2], U32)
        window_attention_stage(nc, T, x, wqkv_aT, bqkv_a, att)
        routing_stage(nc, T, R, "r1", x, wg, table, att, x1)
        expert_stage(nc, T, R, "e1", x1, table, w1, w2)
        projection_stage(nc, T, "cp", x1, wqkv_bT, qk, v)
        attention_stage(nc, T, "at", x1, qk, v, woT, out)
        routing_stage(nc, T, R, "r2", out, wg, table)
        expert_stage(nc, T, R, "e2", out, table, w1, w2)


def kernel(L0_attn_a_hidden_states, L0_attn_a_w_qkv, L0_attn_a_b_qkv, L0_attn_b_w_qkv, L0_attn_b_w_o, L0_ffn_Wg,
           L0_ffn_w1, L0_ffn_w2):
    import numpy as np
    import concourse.bacc as bacc
    from concourse.bass_utils import run_bass_kernel_spmd

    shape = L0_attn_a_hidden_states.shape
    arrays = {
        "x": np.ascontiguousarray(L0_attn_a_hidden_states).reshape(-1, shape[-1]),
        "wqkv_aT": np.ascontiguousarray(np.asarray(L0_attn_a_w_qkv).T),
        "bqkv_a": np.ascontiguousarray(L0_attn_a_b_qkv),
        "wqkv_bT": np.ascontiguousarray(np.asarray(L0_attn_b_w_qkv).T),
        "woT": np.ascontiguousarray(np.asarray(L0_attn_b_w_o).T),
        "wg": np.ascontiguousarray(L0_ffn_Wg),
        "w1": np.ascontiguousarray(L0_ffn_w1),
        "w2": np.ascontiguousarray(L0_ffn_w2),
    }
    nc = bacc.Bacc("TRN2", target_bir_lowering=False, num_devices=1)
    args = [nc.dram_tensor(f"in_{n}", a.shape, mybir.dt.from_np(a.dtype), kind="ExternalInput").ap() for n, a in arrays.items()]
    out = nc.dram_tensor("out_x", arrays["x"].shape, F32, kind="ExternalOutput").ap()
    hybrid_kernel(nc, *args, out)
    result = run_bass_kernel_spmd(nc, [{f"in_{n}": a for n, a in arrays.items()}], core_ids=[0])
    return result.results[0]["out_x"].reshape(shape)
```
